# Optimizing a Trainium2 kernel written in Bass

```python
import numpy as np
import jax
import jax.numpy as jnp

def _softmax(x, axis=-1):
    return jax.nn.softmax(x, axis=axis)

def _gelu(x):
    return jax.nn.gelu(x, approximate=True)

def _silu(x):
    return jax.nn.silu(x)

def _sigmoid(x):
    return jax.nn.sigmoid(x)

def _layernorm(x, axis=-1, eps=1e-05):
    m = jnp.mean(x, axis=axis, keepdims=True)
    v = jnp.var(x, axis=axis, keepdims=True)
    return (x - m) / jnp.sqrt(v + eps)

def _scatter_add(tgt, idx, src, axis=0):
    return tgt.at[idx].add(src)

def _segment_sum(src, seg, n):
    return jax.ops.segment_sum(src, seg, n)
kernel_name = 'mk_adj_preln_d2_adj_r2_57a03e'

def setup_inputs(seed: int=0):
    np.random.seed(seed)
    _w = jnp.asarray

    def _rec_inputs():
        import jax
        import jax.numpy as jnp
        _gk = jax.random.key(seed)
        x = -0.0002928 + 1 * jax.random.normal(jax.random.fold_in(_gk, 1), (8192, 256), jnp.float32)
        _a = jax.random.bernoulli(jax.random.fold_in(_gk, 2), 0.00195312, (8192, 8192))
        _a = jnp.logical_or(_a, jnp.swapaxes(_a, -1, -2))
        _a = jnp.logical_or(_a, jnp.eye(8192, dtype=bool))
        _af = _a.astype(jnp.float32)
        _af = _af * jax.random.uniform(jax.random.fold_in(_gk, 3), (8192, 8192), jnp.float32, 0.05, 5.41998)
        adj = _af
        return (x, adj)
    x, adj = _rec_inputs()

    def _L0_gnn_setup():
        import jax, jax.numpy as jnp
        import numpy as np
        N = 4096
        D = 256
        EPS = 1e-12
        key = jax.random.key(seed)
        k1, k2 = jax.random.split(key)
        cur = jax.random.normal(k1, (N, D), dtype=jnp.float32)
        incidence_m = jax.random.normal(k2, (N, N), dtype=jnp.float32)
        return {'cur': cur, 'incidence_m': incidence_m}
    _L0_gnn_all = _L0_gnn_setup()
    _L0_gnn_in = {k: v for k, v in _L0_gnn_all.items() if k in ()}
    del _L0_gnn_all

    def _L1_gnn_setup():
        import jax, jax.numpy as jnp
        import numpy as np
        N = 8192
        D_IN = 256
        D_OUT = 256
        AVG_DEG = 32.0
        key = jax.random.key(seed)
        k1, k2, k3, k4 = jax.random.split(key, 4)
        p = AVG_DEG / N
        adjacency = (jax.random.uniform(k1, (N, N)) < p).astype(jnp.float32)
        adjacency = jnp.maximum(adjacency, adjacency.T)
        node_degree = jnp.sum(adjacency, axis=1, keepdims=True) + 1.0
        x = jax.random.normal(k2, (N, D_IN), dtype=jnp.float32)
        W = jax.random.normal(k3, (D_IN, D_OUT), dtype=jnp.float32) * (1.0 / np.sqrt(D_IN))
        b = jax.random.normal(k4, (D_OUT,), dtype=jnp.float32) * 0.01
        return {'x': x, 'adjacency': adjacency, 'node_degree': node_degree, 'W': W, 'b': b}
    _L1_gnn_all = _L1_gnn_setup()
    _L1_gnn_in = {k: v for k, v in _L1_gnn_all.items() if k in ('W', 'b')}
    del _L1_gnn_all
    return {'x': x, 'adj': adj, 'L1_gnn_W': _L1_gnn_in['W'], 'L1_gnn_b': _L1_gnn_in['b']}

def reference(x, adj, L1_gnn_W, L1_gnn_b):
    import jax
    import jax.numpy as jnp

    def _L0_gnn_ref(cur, incidence_m):
        import jax, jax.numpy as jnp
        import numpy as np
        N = 4096
        D = 256
        EPS = 1e-12
        mask = incidence_m > 0
        head = jax.lax.stop_gradient(mask.astype(incidence_m.dtype))
        head = head / jnp.maximum(jnp.sqrt(jnp.sum(head * head, axis=-1, keepdims=True)), EPS)
        inc = incidence_m + head
        edge_fea = inc @ cur
        edge_degree = jnp.sum(inc, axis=-1, keepdims=True)
        return edge_fea / edge_degree

    def _L1_gnn_ref(x, adjacency, node_degree, W, b):
        import jax, jax.numpy as jnp
        import numpy as np
        N = 8192
        D_IN = 256
        D_OUT = 256
        AVG_DEG = 32.0
        n = adjacency.shape[0]
        a_hat = adjacency + jnp.eye(n, dtype=adjacency.dtype)
        dinv = jax.lax.rsqrt(node_degree)
        a_norm = dinv * a_hat * dinv
        pooled = a_norm @ x + x
        return jax.nn.relu(pooled @ W + b)
    deg = jnp.maximum((adj != 0).astype(jnp.float32).sum(-1), 1.0)
    h = jnp.maximum(_layernorm(x, axis=-1), 0.0)
    x = x + _L0_gnn_ref(h, adj)
    h = jnp.maximum(_layernorm(x, axis=-1), 0.0)
    x = x + _L1_gnn_ref(h, adj, deg[..., None], L1_gnn_W, L1_gnn_b)
    return x

_drawn_inputs = setup_inputs


def setup_inputs(seed=0):
    import zlib

    import numpy as np

    out = dict(_drawn_inputs(seed))
    spreads = {}
    factors = {'L1_gnn_b': 8.0}
    for name, (base, spread) in spreads.items():
        noise = np.random.default_rng([zlib.crc32(name.encode()), seed]).standard_normal(out[name].shape)
        drawn = base * np.exp(spread * noise) if base else spread * noise
        out[name] = jnp.asarray(drawn.astype(out[name].dtype))
    for name, factor in factors.items():
        out[name] = (out[name] * factor).astype(out[name].dtype)
    return out
```

```python
import concourse.bass as bass
from concourse import mybir
from contextlib import ExitStack


def gnn_two_layer_kernel(
    nc: bass.Bass,
    x: bass.AP,
    adj_t: bass.AP,
    w: bass.AP,
    b: bass.AP,
    out: bass.AP,
):
    fp32, fp16, u32 = mybir.dt.float32, mybir.dt.float16, mybir.dt.uint32
    ALU = mybir.AluOpType
    ACT = mybir.ActivationFunctionType
    AX = mybir.AxisListType

    P = 128
    N, D = x.shape
    UNITS = N // P
    KT = N // P
    CHUNKS = 4
    SUBS = 8
    KPC, KPS = KT // CHUNKS, KT // SUBS
    CW, SW = KPC * P, KPS * P
    RAW = 2 * CHUNKS
    RING = 4
    GT = KT // CHUNKS
    GX = KT // SUBS
    HS = 2048.0
    LN_EPS, NORM_EPS = 1e-5, 1e-12
    HW = 2 * D + 2

    x_tiles = x.rearrange("(t p) d -> t p d", p=P)
    x_groups = x.rearrange("(g t p) d -> g p t d", p=P, t=GX)
    out_tiles = out.rearrange("(t p) d -> t p d", p=P)
    adj_rows = adj_t.rearrange("u c p f -> (u c p) f")
    x1_dram = nc.dram_tensor("x1_dram", [N, D], fp32, kind="Internal").ap()
    g_dram = nc.dram_tensor("g_dram", [N, 2 * D], fp16, kind="Internal").ap()
    g_groups = g_dram.rearrange("(g t p) d -> g p t d", p=P, t=GT)

    ctx = ExitStack()
    with ctx:
        def sb(name, shape, dt):
            return ctx.enter_context(nc.sbuf_tensor(name, shape, dt))

        def pb(name):
            return ctx.enter_context(nc.psum_tensor(name, [P, 512], fp32))

        def sem(name):
            return ctx.enter_context(nc.semaphore(name))

        H = sb("H", [P, KT, HW], fp16)
        raw = sb("raw", [P, RAW, CW], fp32)
        a_hi = sb("a_hi", [P, RING, SW], fp16)
        a_lo = sb("a_lo", [P, RING, SW], fp16)
        a_pos = sb("a_pos", [P, RING, SW], fp16)
        nz_acc = sb("nz_acc", [P, 2, SW], fp16)
        junk = sb("junk", [P, 2, CW], mybir.dt.bfloat16)
        xg = sb("xg", [P, 2, GX, D], fp32)
        zt = sb("zt", [P, 2, D], fp32)
        stats = sb("stats", [P, GX, 6], fp32)
        mv = sb("mv", [P, GX, 2], fp32)
        sd = sb("sd", [P, GX], fp32)
        nt = sb("nt", [P, GX], fp32)
        rs = sb("rs", [P, GX], fp32)
        asum = sb("asum", [P, 2, CHUNKS], fp32)
        amax = sb("amax", [P, 2, CHUNKS], fp32)
        am = sb("am", [P, 1], fp32)
        ebits = sb("ebits", [P, 1], u32)
        scale = sb("scale", [P, UNITS], fp32)
        sc_now = sb("sc_now", [P, 2], fp32)
        un_now = sb("un_now", [P, 2], fp32)
        mv1 = sb("mv1", [P, 2], fp32)
        mean_t = sb("mean_t", [P, UNITS], fp32)
        rstd_t = sb("rstd_t", [P, UNITS], fp32)
        agg_t = sb("agg_t", [P, UNITS], fp32)
        self_t = sb("self_t", [P, UNITS], fp32)
        cnt = sb("cnt", [P, 2], fp32)
        cnt_sq = sb("cnt_sq", [P, 2], fp32)
        cnt_r = sb("cnt_r", [P, 2], fp32)
        cnt_n = sb("cnt_n", [P, 2], fp32)
        deg_r = sb("deg_r", [P, 1], fp32)
        ve = sb("ve", [P, 1], fp32)
        ve_s = sb("ve_s", [P, 1], fp32)
        ve_r = sb("ve_r", [P, 1], fp32)
        ve_n = sb("ve_n", [P, 1], fp32)
        rden = sb("rden", [P, 1], fp32)
        rs_g = sb("rs_g", [P, 1], fp32)
        st1 = sb("st1", [P, 6], fp32)
        x_in = sb("x_in", [P, 2, D], fp32)
        x1_o = sb("x1_o", [P, 2, D], fp32)
        g_o = sb("g_o", [P, 2, 2 * D], fp16)
        agg = sb("agg", [P, D + 1], fp32)
        num = sb("num", [P, D + 1], fp32)
        z1 = sb("z1", [P, D], fp32)
        hc = sb("hc", [P, D], fp32)
        pooled = sb("pooled", [P, D], fp32)
        pooled_t = sb("pooled_t", [P, D], fp32)
        y = sb("y", [P, D], fp32)
        w_sb = sb("w_sb", [P, D // P, D], fp32)
        b_sb = sb("b_sb", [P, D], fp32)
        ones = sb("ones", [P, 1], fp16)
        ident = sb("ident", [P, P], fp32)

        ps_a = [pb("ps_a0"), pb("ps_a1")]
        ps_m = [pb("ps_m0"), pb("ps_m1")]
        ps_n = pb("ps_n")
        ps_t = pb("ps_t")
        ps_o = pb("ps_o")

        raw_in = [sem(f"raw_in{i}") for i in range(RAW)]
        xg_in = [sem("xg_in0"), sem("xg_in1")]
        x_got = [sem("x_got0"), sem("x_got1")]
        x1_st = [sem("x1_st0"), sem("x1_st1")]
        g_st = [sem("g_st0"), sem("g_st1")]
        g_in = [sem(f"g_in{i}") for i in range(CHUNKS)]
        w_in = sem("w_in")
        const_set = sem("const_set")
        ident0 = sem("ident0")
        ones_h = sem("ones_h")
        ln_mv = sem("ln_mv")
        ln_sd = sem("ln_sd")
        ln_step = sem("ln_step")
        z_done = sem("z_done")
        h_hi = sem("h_hi")
        h_done = sem("h_done")
        asum_done = sem("asum_done")
        amax_done = sem("amax_done")
        sc_step = sem("sc_step")
        scale_done = sem("scale_done")
        hi_done = sem("hi_done")
        pos_done = sem("pos_done")
        nz_done = sem("nz_done")
        lo_done = sem("lo_done")
        sub_done = sem("sub_done")
        unit_done = sem("unit_done")
        cnt_done = sem("cnt_done")
        cnt_root = sem("cnt_root")
        agg_done = sem("agg_done")
        num_done = sem("num_done")
        ep_step = sem("ep_step")
        x1_done = sem("x1_done")
        deg_done = sem("deg_done")
        ve_done = sem("ve_done")
        ve_root = sem("ve_root")
        g_done = sem("g_done")
        pool_done = sem("pool_done")
        tp_done = sem("tp_done")
        tc_done = sem("tc_done")
        o_done = sem("o_done")
        y_done = sem("y_done")
        res_done = sem("res_done")
        fin_step = sem("fin_step")

        block = ctx.enter_context(nc.Block())

        def sub_at(slot, s):
            return raw[:, slot + s // 2, (s % 2) * SW:(s % 2 + 1) * SW]

        def is_zero(u):
            return isinstance(u, int) and u == 0

        @block.sync
        def _(sp):
            def load_chunk(v, j, src_unit, par, first=False):
                if not first:
                    sp.wait_ge(lo_done, SUBS * (v - 2) + 2 * j + 2)
                row = (src_unit * CHUNKS + j) * P
                sp.dma_start(raw[:, CHUNKS * par + j, :], adj_rows[bass.ds(row, P), :])\
                    .then_inc(raw_in[CHUNKS * par + j], 16)

            def load_xg(g):
                if g >= 2:
                    sp.wait_ge(z_done, GX * (g - 1))
                sp.dma_start(xg[:, g % 2, :, :], x_groups[g]).then_inc(xg_in[g % 2], 16)

            load_xg(0)
            for j in range(CHUNKS):
                load_chunk(0, j, 0, 0, True)
                if j == 0:
                    load_xg(1)
            sp.dma_start(w_sb[:, :, :], w.rearrange("(c p) n -> p c n", p=P)).then_inc(w_in, 16)
            sp.dma_start(b_sb[:, :], b.partition_broadcast(P)).then_inc(w_in, 16)
            load_xg(2)
            for j in range(CHUNKS):
                load_chunk(1, j, 1, 1, True)
            sp.dma_start(x_in[:, 0, :], x_tiles[0]).then_inc(x_got[0], 16)
            for g in range(3, SUBS):
                load_xg(g)

            def step0(u, par, first=False, wrap=False, last=False):
                for j in range(CHUNKS):
                    load_chunk(u + 2, j, u + 2 - UNITS if wrap else u + 2, par)
                if not first:
                    store0(u - 1, 1 - par)
                if not last:
                    sp.dma_start(x_in[:, 1 - par, :], x[bass.ds((u + 1) * P, P), :]).then_inc(x_got[1 - par], 16)

            def store0(u, par):
                sp.wait_ge(x1_done, u + 1)
                sp.dma_start(x1_dram[bass.ds(u * P, P), :], x1_o[:, par, :]).then_inc(x1_st[par], 16)
                sp.wait_ge(g_done, u + 1)
                sp.dma_start(g_dram[bass.ds(u * P, P), :], g_o[:, par, :]).then_inc(g_st[par], 16)

            step0(0, 0, first=True)
            with nc.sync.Fori(0, (UNITS - 4) // 2) as i:
                for r in range(2):
                    step0(2 * i + 1 + r, (1 + r) % 2)
            step0(UNITS - 3, 1)
            step0(UNITS - 2, 0, wrap=True)
            step0(UNITS - 1, 1, wrap=True, last=True)

            for g in range(CHUNKS):
                if g == CHUNKS - 1:
                    store0(UNITS - 1, 1)
                sp.wait_ge(sub_done, SUBS * (UNITS - 1) + 2 * g + 2)
                for par in range(2):
                    sp.wait_ge(g_st[par], 16 * (GT * (g + 1) // 2))
                sp.dma_start(H[:, g * GT:(g + 1) * GT, 0:2 * D], g_groups[g]).then_inc(g_in[g], 16)
            for par in range(2):
                sp.wait_ge(x1_st[par], 16 * (UNITS // 2))
                sp.dma_start(x_in[:, par, :], x1_dram[par * P:(par + 1) * P, :]).then_inc(x_got[par], 16)

            def step1(u, par, first=False, more=True, last=False):
                if more:
                    for j in range(CHUNKS):
                        load_chunk(UNITS + u + 2, j, u + 2, par)
                if not first:
                    store1(u - 1, 1 - par)
                    if not last:
                        sp.dma_start(x_in[:, 1 - par, :], x1_dram[bass.ds((u + 1) * P, P), :])\
                            .then_inc(x_got[1 - par], 16)

            def store1(u, par):
                sp.wait_ge(res_done, u + 1)
                sp.dma_start(out[bass.ds(u * P, P), :], x1_o[:, par, :]).then_inc(x1_st[par], 16)

            step1(0, 0, first=True)
            with nc.sync.Fori(0, (UNITS - 4) // 2) as i:
                for r in range(2):
                    step1(2 * i + 1 + r, (1 + r) % 2)
            step1(UNITS - 3, 1)
            step1(UNITS - 2, 0, more=False)
            step1(UNITS - 1, 1, more=False, last=True)
            store1(UNITS - 1, 1)
            for par in range(2):
                sp.wait_ge(x1_st[par], 16 * UNITS)
                sp.wait_ge(g_st[par], 16 * (UNITS // 2))

        @block.gpsimd
        def _(pool):
            nc.gpsimd.memset(ident[:, :], 0.0).then_inc(ident0, 1)
            nc.gpsimd.memset(ones[:, :], 1.0).then_inc(const_set, 1)
            nc.gpsimd.memset(H[:, :, 2 * D:2 * D + 1], HS).then_inc(ones_h, 1)
            pool.wait_ge(ident0, 1)
            nc.gpsimd.affine_select(out=ident[:, :], in_=ident[:, :], compare_op=ALU.not_equal, fill=1.0,
                                    base=0, pattern=[[-1, P]], channel_multiplier=1).then_inc(const_set, 1)

            def spread(u, par):
                pool.wait_ge(asum_done, CHUNKS * (u + 1))
                nc.gpsimd.partition_all_reduce(amax[:, par, :], asum[:, par, :], P,
                                               bass.bass_isa.ReduceOp.max).then_inc(amax_done, 1)

            for u in range(UNITS):
                spread(u, u % 2)

        @block.scalar
        def _(act):
            def chunk_sum(u, par, j, uses):
                act.wait_ge(raw_in[CHUNKS * par + j], 16 * uses)
                if not (is_zero(u) and j < 2):
                    act.wait_ge(asum_done, CHUNKS * u + j - 1)
                nc.scalar.activation(junk[:, j % 2, :], raw[:, CHUNKS * par + j, :], ACT.Abs,
                                     accum_out=asum[:, par, j:j + 1]).then_inc(asum_done, 1)

            def split_hi(v, u, par, s, free=True):
                if free:
                    act.wait_ge(sub_done, SUBS * v + s - RING + 1)
                nc.scalar.activation(a_hi[:, s % RING, :], sub_at(CHUNKS * par, s), ACT.Copy,
                                     scale=sc_now[:, par:par + 1]).then_inc(hi_done, 1)

            for j in range(CHUNKS):
                chunk_sum(0, 0, j, 1)
            for g in range(KT // GX):
                act.wait_ge(ln_mv, g + 1)
                nc.scalar.activation(sd[:, :], nt[:, :], ACT.Sqrt).then_inc(ln_sd, 1)
                for t in range(GX):
                    n = g * GX + t
                    act.wait_ge(z_done, n + 1)
                    nc.scalar.activation(H[:, n, D:2 * D], zt[:, n % 2, :], ACT.Relu).then_inc(h_hi, 1)

            def epilogue0(u, par):
                act.wait_ge(cnt_done, u + 1)
                nc.scalar.activation(cnt_sq[:, :], cnt[:, :], ACT.Sqrt).then_inc(cnt_root, 1)
                act.wait_ge(unit_done, u + 1)
                if not is_zero(u):
                    act.wait_ge(num_done, u)
                nc.scalar.activation(agg[:, :], ps_a[par][:, 0:D + 1], ACT.Copy,
                                     scale=un_now[:, par:par + 1]).then_inc(agg_done, 1)
                act.wait_ge(ve_done, u + 1)
                nc.scalar.activation(ve_s[:, :], ve[:, :], ACT.Sqrt).then_inc(ve_root, 1)

            def step0(u, par, pair, first=False, last=False):
                act.wait_ge(scale_done, u + 1)
                for s in range(SUBS):
                    split_hi(u, u, par, s, free=not (first and s < RING))
                    if s == RING - 1 and not first:
                        epilogue0(u - 1, 1 - par)
                    if 1 <= s <= CHUNKS and not last:
                        chunk_sum(u + 1, 1 - par, s - 1, pair)

            step0(0, 0, 1, first=True)
            step0(1, 1, 2)
            step0(2, 0, 2)
            with nc.scalar.Fori(1, UNITS // 2 - 1) as i:
                for r in range(2):
                    step0(2 * i + 1 + r, (1 + r) % 2, i + 2)
            step0(UNITS - 1, 1, UNITS // 2, last=True)

            def step1(u, par, uses, first=False):
                act.wait_ge(scale_done, UNITS + u + 1)
                for s in range(SUBS):
                    if s % 2 == 0:
                        act.wait_ge(raw_in[CHUNKS * par + s // 2], 16 * uses)
                    split_hi(UNITS + u, u, par, s)
                    if s == RING - 1 and first:
                        epilogue0(UNITS - 1, 1)
                    if s == 6 and not first:
                        turn(u - 1)

            def turn(u):
                act.wait_ge(tp_done, u + 1)
                if not is_zero(u):
                    act.wait_ge(o_done, u)
                nc.scalar.activation(pooled_t[:, :], ps_t[:, 0:D], ACT.Copy).then_inc(tc_done, 1)

            step1(0, 0, UNITS // 2 + 1, first=True)
            step1(1, 1, UNITS // 2 + 1)
            step1(2, 0, UNITS // 2 + 2)
            with nc.scalar.Fori(1, UNITS // 2 - 1) as i:
                for r in range(2):
                    step1(2 * i + 1 + r, (1 + r) % 2, UNITS // 2 + i + 1 + r)
            step1(UNITS - 1, 1, UNITS)
            turn(UNITS - 1)

        @block.vector
        def _(dve):
            steps = [0]

            def link(ins, step_sem, count):
                ins.then_inc(step_sem, 1)
                dve.wait_ge(step_sem, count)

            for g in range(KT // GX):
                dve.wait_ge(xg_in[g % 2], 16 * (g // 2 + 1))
                for t in range(GX):
                    last = nc.vector.bn_stats(stats[:, t, :], xg[:, g % 2, t, :])
                link(last, ln_step, 3 * g + 1 + g * 4)
                for t in range(GX):
                    last = nc.vector.bn_aggr(mv[:, t, :], stats[:, t, :])
                link(last, ln_step, 3 * g + 2 + g * 4)
                link(nc.vector.tensor_scalar(nt[:, :], mv[:, :, 1], LN_EPS, None, ALU.add), ln_mv, g + 1)
                dve.wait_ge(ln_sd, g + 1)
                link(nc.vector.reciprocal(rs[:, :], sd[:, :]), ln_step, 3 * g + 3 + g * 4)
                link(nc.vector.tensor_tensor(sd[:, :], nt[:, :], rs[:, :], ALU.mult), ln_step, 3 * g + 4 + g * 4)
                link(nc.vector.tensor_tensor(sd[:, :], sd[:, :], rs[:, :], ALU.mult), ln_step, 3 * g + 5 + g * 4)
                link(nc.vector.tensor_scalar(sd[:, :], sd[:, :], -0.5 * HS, 1.5 * HS, ALU.mult, ALU.add),
                     ln_step, 3 * g + 6 + g * 4)
                link(nc.vector.tensor_tensor(rs[:, :], rs[:, :], sd[:, :], ALU.mult), ln_step, 3 * g + 7 + g * 4)

                def normal(t):
                    n = g * GX + t
                    if n >= 2:
                        dve.wait_ge(h_hi, n - 1)
                        dve.wait_ge(h_done, n - 1)
                    nc.vector.tensor_scalar(zt[:, n % 2, :], xg[:, g % 2, t, :], mv[:, t, 0:1], rs[:, t:t + 1],
                                            ALU.subtract, ALU.mult).then_inc(z_done, 1)

                def h_lo(t):
                    n = g * GX + t
                    dve.wait_ge(h_hi, n + 1)
                    nc.vector.scalar_tensor_tensor(out=H[:, n, 0:D], in0=zt[:, n % 2, :], scalar=0.0,
                                                   in1=H[:, n, D:2 * D], op0=ALU.max, op1=ALU.subtract)\
                        .then_inc(h_done, 1)

                normal(0)
                for t in range(1, GX):
                    normal(t)
                    h_lo(t - 1)
                h_lo(GX - 1)

            def find_scale(u, par):
                base = 3 * u
                dve.wait_ge(amax_done, u + 1)
                link(nc.vector.reduce_max(am[:, :], amax[:, par, :], AX.X), sc_step, base + 1)
                link(nc.vector.tensor_scalar(ebits[:, :], am[:, :].bitcast(u32), 0x7F800000, None,
                                             ALU.bitwise_and), sc_step, base + 2)
                link(nc.vector.tensor_scalar(ebits[:, :], ebits[:, :], float(15 << 23), None, ALU.max),
                     sc_step, base + 3)
                nc.vector.tensor_scalar(un_now[:, par:par + 1].bitcast(u32), ebits[:, :],
                                        -float(14 << 23), None, ALU.add)
                link(nc.vector.tensor_scalar(sc_now[:, par:par + 1].bitcast(u32), ebits[:, :], -1.0,
                                             float(268 << 23), ALU.mult, ALU.add), scale_done, u + 1)
                nc.vector.tensor_copy(scale[:, bass.ds(u, 1)], sc_now[:, par:par + 1])

            find_scale(0, 0)

            def split_lo(v, u, par, s):
                dve.wait_ge(hi_done, SUBS * v + s + 1)
                nc.vector.scalar_tensor_tensor(out=a_lo[:, s % RING, :], in0=sub_at(CHUNKS * par, s),
                                               scalar=sc_now[:, par:par + 1], in1=a_hi[:, s % RING, :],
                                               op0=ALU.mult, op1=ALU.subtract).then_inc(lo_done, 1)

            def masks(u, par, s, uses, free=True):
                if s % 2 == 0:
                    dve.wait_ge(raw_in[CHUNKS * par + s // 2], 16 * uses)
                if free:
                    dve.wait_ge(sub_done, SUBS * u + s - RING + 1)
                src = sub_at(CHUNKS * par, s)
                nc.vector.tensor_scalar(a_pos[:, s % RING, :], src, 0.0, None, ALU.is_gt).then_inc(pos_done, 1)
                if s == 0:
                    nc.vector.tensor_scalar(nz_acc[:, par, :], src, 0.0, None, ALU.not_equal)\
                        .then_inc(nz_done, 1)
                else:
                    dve.wait_ge(nz_done, SUBS * u + s)
                    nc.vector.scalar_tensor_tensor(out=nz_acc[:, par, :], in0=src, scalar=0.0,
                                                   in1=nz_acc[:, par, :], op0=ALU.not_equal, op1=ALU.add)\
                        .then_inc(nz_done, 1)

            EP = 13

            def epilogue0(u, par, uses):
                base = EP * u
                PA, PM = ps_a[par], ps_m[par]
                dve.wait_ge(unit_done, u + 1)
                nc.vector.tensor_scalar(cnt[:, 0:1], PM[:, D:D + 1], 1.0 / HS, None, ALU.mult)
                link(nc.vector.tensor_scalar(cnt[:, 1:2], ps_n[:, 8 * par:8 * par + 1], 1.0, None, ALU.max),
                     cnt_done, u + 1)
                dve.wait_ge(cnt_root, u + 1)
                link(nc.vector.tensor_scalar(cnt_sq[:, :], cnt_sq[:, :], NORM_EPS, None, ALU.max),
                     ep_step, base + 1)
                link(nc.vector.reciprocal(cnt_r[:, :], cnt_sq[:, :]), ep_step, base + 2)
                link(nc.vector.tensor_tensor(cnt_n[:, :], cnt[:, :], cnt_r[:, :], ALU.mult), ep_step, base + 3)
                link(nc.vector.tensor_tensor(cnt_n[:, :], cnt_n[:, :], cnt_r[:, :], ALU.mult), ep_step, base + 4)
                link(nc.vector.tensor_scalar(cnt_n[:, :], cnt_n[:, :], -0.5, 1.5, ALU.mult, ALU.add),
                     ep_step, base + 5)
                link(nc.vector.tensor_tensor(cnt_r[:, :], cnt_r[:, :], cnt_n[:, :], ALU.mult), ep_step, base + 6)
                dve.wait_ge(agg_done, u + 1)
                link(nc.vector.scalar_tensor_tensor(out=num[:, :], in0=PM[:, 0:D + 1], scalar=cnt_r[:, 0:1],
                                                    in1=agg[:, :], op0=ALU.mult, op1=ALU.add), num_done, u + 1)
                link(nc.vector.reciprocal(rden[:, :], num[:, D:D + 1]), ep_step, base + 7)
                dve.wait_ge(x_got[par], 16 * uses)
                if not (isinstance(uses, int) and uses == 1):
                    dve.wait_ge(x1_st[par], 16 * (uses - 1))
                link(nc.vector.scalar_tensor_tensor(out=x1_o[:, par, :], in0=num[:, 0:D], scalar=rden[:, :],
                                                    in1=x_in[:, par, :], op0=ALU.mult, op1=ALU.add),
                     x1_done, u + 1)
                link(nc.vector.bn_stats(st1[:, :], x1_o[:, par, :]), ep_step, base + 8)
                nc.vector.tensor_scalar(deg_r[:, :], cnt_r[:, 1:2], cnt_r[:, 1:2], 1.0 / HS, ALU.mult, ALU.mult)\
                    .then_inc(deg_done, 1)
                nc.vector.tensor_scalar(self_t[:, bass.ds(u, 1)], cnt_r[:, 1:2], cnt_r[:, 1:2], 1.0,
                                        ALU.mult, ALU.add)
                link(nc.vector.bn_aggr(mv1[:, :], st1[:, :]), ep_step, base + 9)
                nc.vector.tensor_copy(mean_t[:, bass.ds(u, 1)], mv1[:, 0:1])
                link(nc.vector.tensor_scalar(ve[:, :], mv1[:, 1:2], LN_EPS, None, ALU.add),
                     ve_done, u + 1)
                dve.wait_ge(deg_done, u + 1)
                nc.vector.tensor_tensor(agg_t[:, bass.ds(u, 1)], deg_r[:, :], un_now[:, par:par + 1], ALU.mult)
                dve.wait_ge(ve_root, u + 1)
                link(nc.vector.reciprocal(ve_r[:, :], ve_s[:, :]), ep_step, base + 10)
                link(nc.vector.scalar_tensor_tensor(out=ve_n[:, :], in0=ve[:, :], scalar=ve_r[:, :],
                                                    in1=ve_r[:, :], op0=ALU.mult, op1=ALU.mult),
                     ep_step, base + 11)
                link(nc.vector.tensor_scalar(ve_n[:, :], ve_n[:, :], -0.5, 1.5, ALU.mult, ALU.add),
                     ep_step, base + 12)
                link(nc.vector.tensor_tensor(rstd_t[:, bass.ds(u, 1)], ve_r[:, :], ve_n[:, :], ALU.mult),
                     ep_step, base + 13)
                finish0(u, par, uses)

            def finish0(u, par, uses):
                base = 3 * u
                link(nc.vector.tensor_scalar(rs_g[:, :], rstd_t[:, bass.ds(u, 1)], HS, None, ALU.mult), fin_step, base + 1)
                link(nc.vector.tensor_scalar(z1[:, :], x1_o[:, par, :], mv1[:, 0:1], rs_g[:, :],
                                             ALU.subtract, ALU.mult), fin_step, base + 2)
                if not (isinstance(uses, int) and uses == 1):
                    dve.wait_ge(g_st[par], 16 * (uses - 1))
                link(nc.vector.tensor_scalar(g_o[:, par, D:2 * D], z1[:, :], 0.0, None, ALU.max),
                     fin_step, base + 3)
                nc.vector.scalar_tensor_tensor(out=g_o[:, par, 0:D], in0=z1[:, :], scalar=0.0,
                                               in1=g_o[:, par, D:2 * D], op0=ALU.max, op1=ALU.subtract)\
                    .then_inc(g_done, 1)

            def step0(u, par, uses, first=False, last=False, ep_uses=1):
                for s in range(SUBS):
                    masks(u, par, s, uses, free=not (first and s < RING))
                    split_lo(u, u, par, s)
                    if s == RING - 1 and not first:
                        epilogue0(u - 1, 1 - par, ep_uses)
                    if s == CHUNKS + 1 and not last:
                        find_scale(u + 1, 1 - par)

            step0(0, 0, 1, first=True)
            step0(1, 1, 1, ep_uses=1)
            step0(2, 0, 2, ep_uses=1)
            with nc.vector.Fori(1, UNITS // 2 - 1) as i:
                step0(2 * i + 1, 1, i + 1, ep_uses=i + 1)
                step0(2 * i + 2, 0, i + 2, ep_uses=i + 1)
            step0(UNITS - 1, 1, UNITS // 2, last=True, ep_uses=UNITS // 2)

            def pool_row(u, par, uses):
                dve.wait_ge(x_got[par], 16 * uses)
                link(nc.vector.tensor_scalar(z1[:, :], x_in[:, par, :], mean_t[:, bass.ds(u, 1)],
                                             rstd_t[:, bass.ds(u, 1)], ALU.subtract, ALU.mult),
                     fin_step, 3 * UNITS + 2 * u + 1)
                link(nc.vector.tensor_scalar(hc[:, :], z1[:, :], 0.0, self_t[:, bass.ds(u, 1)], ALU.max, ALU.mult),
                     fin_step, 3 * UNITS + 2 * u + 2)
                dve.wait_ge(unit_done, UNITS + u + 1)
                if not is_zero(u):
                    dve.wait_ge(tp_done, u)
                nc.vector.scalar_tensor_tensor(out=pooled[:, :], in0=ps_a[par][:, 0:D],
                                               scalar=agg_t[:, bass.ds(u, 1)], in1=hc[:, :],
                                               op0=ALU.mult, op1=ALU.add).then_inc(pool_done, 1)

            def result(u, par, uses):
                dve.wait_ge(o_done, u + 1)
                link(nc.vector.tensor_tensor(y[:, :], ps_o[:, 0:D], b_sb[:, :], ALU.add), y_done, u + 1)
                dve.wait_ge(x1_st[par], 16 * (uses - 1))
                nc.vector.scalar_tensor_tensor(out=x1_o[:, par, :], in0=y[:, :], scalar=0.0,
                                               in1=x_in[:, par, :], op0=ALU.max, op1=ALU.add)\
                    .then_inc(res_done, 1)

            def step1(u, par, uses, first=False, ep_uses=None):
                if not first:
                    dve.wait_ge(hi_done, SUBS * (UNITS + u - 1))
                nc.vector.tensor_copy(sc_now[:, par:par + 1], scale[:, bass.ds(u, 1)]).then_inc(scale_done, 1)
                dve.wait_ge(scale_done, UNITS + u + 1)
                for s in range(SUBS):
                    if s % 2 == 0:
                        dve.wait_ge(raw_in[CHUNKS * par + s // 2], 16 * uses)
                    dve.wait_ge(sub_done, SUBS * (UNITS + u) + s - RING + 1)
                    split_lo(UNITS + u, u, par, s)
                    if s == RING - 1:
                        if first:
                            epilogue0(UNITS - 1, 1, UNITS // 2)
                        else:
                            pool_row(u - 1, 1 - par, ep_uses)
                    if s == SUBS - 2 and not first:
                        result(u - 1, 1 - par, ep_uses)

            dve.wait_ge(w_in, 32)
            half = UNITS // 2
            step1(0, 0, half + 1, first=True)
            step1(1, 1, half + 1, ep_uses=half + 1)
            step1(2, 0, half + 2, ep_uses=half + 1)
            with nc.vector.Fori(1, half - 1) as i:
                step1(2 * i + 1, 1, half + i + 1, ep_uses=half + i + 1)
                step1(2 * i + 2, 0, half + i + 2, ep_uses=half + i + 1)
            step1(UNITS - 1, 1, UNITS, ep_uses=UNITS)
            pool_row(UNITS - 1, 1, UNITS)
            result(UNITS - 1, 1, UNITS)

        @block.tensor
        def _(pe):
            pe.wait_ge(ones_h, 1)
            pe.wait_ge(const_set, 2)

            def unit0(u, par, first=False, free=True):
                if free:
                    pe.wait_ge(agg_done, u - 1)
                    pe.wait_ge(num_done, u - 1)
                PA, PM = ps_a[par], ps_m[par]
                for s in range(SUBS):
                    pe.wait_ge(hi_done, SUBS * u + s + 1)
                    pe.wait_ge(lo_done, SUBS * u + s + 1)
                    for k in range(KPS):
                        kt = s * KPS + k
                        if first:
                            pe.wait_ge(h_done, kt + 1)
                        hi = a_hi[:, s % RING, k * P:(k + 1) * P]
                        lo = a_lo[:, s % RING, k * P:(k + 1) * P]
                        pos = a_pos[:, s % RING, k * P:(k + 1) * P]
                        h_hi1, h_lo = H[:, kt, D:2 * D + 1], H[:, kt, 0:D]
                        nc.tensor.matmul(PA[:, 0:D + 1], hi, h_hi1, start=(kt == 0), stop=False)
                        nc.tensor.matmul(PA[:, 0:D], hi, h_lo, start=False, stop=False)
                        nc.tensor.matmul(PA[:, 0:D + 1], lo, h_hi1, start=False, stop=(kt == KT - 1))
                        nc.tensor.matmul(PM[:, 0:D + 1], pos, h_hi1, start=(kt == 0), stop=False)
                        last = nc.tensor.matmul(PM[:, 0:D], pos, h_lo, start=False, stop=(kt == KT - 1))
                    last.then_inc(sub_done, 1)
                pe.wait_ge(nz_done, SUBS * (u + 1))
                for k in range(KPS):
                    last = nc.tensor.matmul(ps_n[:, 8 * par:8 * par + 1], nz_acc[:, par, k * P:(k + 1) * P],
                                            ones[:, :], start=(k == 0), stop=(k == KPS - 1))
                last.then_inc(unit_done, 1)

            unit0(0, 0, first=True, free=False)
            unit0(1, 1, free=False)
            with nc.tensor.Fori(1, UNITS // 2) as i:
                for r in range(2):
                    unit0(2 * i + r, r)

            def turn(u):
                pe.wait_ge(pool_done, u + 1)
                for c in range(D // P):
                    last = nc.tensor.transpose(ps_t[:, c * P:(c + 1) * P], pooled[:, c * P:(c + 1) * P], ident[:, :])
                last.then_inc(tp_done, 1)

            def dense(u):
                pe.wait_ge(tc_done, u + 1)
                if not is_zero(u):
                    pe.wait_ge(y_done, u)
                for c in range(D // P):
                    last = nc.tensor.matmul(ps_o[:, 0:D], pooled_t[:, c * P:(c + 1) * P], w_sb[:, c, :],
                                            start=(c == 0), stop=(c == D // P - 1))
                last.then_inc(o_done, 1)

            def unit1(u, par, first=False, free=True):
                if first and free:
                    pe.wait_ge(agg_done, UNITS - 1)
                    pe.wait_ge(num_done, UNITS - 1)
                elif free:
                    pe.wait_ge(pool_done, u - 1)
                PA = ps_a[par]
                for s in range(SUBS):
                    if first and s % 2 == 0:
                        pe.wait_ge(g_in[s // 2], 16)
                    pe.wait_ge(lo_done, SUBS * (UNITS + u) + s + 1)
                    pe.wait_ge(hi_done, SUBS * (UNITS + u) + s + 1)
                    for k in range(KPS):
                        kt = s * KPS + k
                        hi = a_hi[:, s % RING, k * P:(k + 1) * P]
                        lo = a_lo[:, s % RING, k * P:(k + 1) * P]
                        nc.tensor.matmul(PA[:, 0:D], hi, H[:, kt, D:2 * D], start=(kt == 0), stop=False)
                        nc.tensor.matmul(PA[:, 0:D], hi, H[:, kt, 0:D], start=False, stop=False)
                        last = nc.tensor.matmul(PA[:, 0:D], lo, H[:, kt, D:2 * D], start=False,
                                                stop=(kt == KT - 1))
                    last.then_inc(sub_done, 1)
                    if s == 2 and not first:
                        turn(u - 1)
                    if s == 4 and not first:
                        dense(u - 1)

            def close1(u):
                nc.tensor.matmul(ps_n[0:1, 16:17], ones[:, :], ones[:, :], start=True, stop=True)\
                    .then_inc(unit_done, 1)

            pe.wait_ge(w_in, 32)
            unit1(0, 0, first=True)
            close1(0)
            pe.wait_ge(agg_done, UNITS)
            pe.wait_ge(num_done, UNITS)
            unit1(1, 1, free=False)
            close1(1)
            with nc.tensor.Fori(1, UNITS // 2) as i:
                for r in range(2):
                    unit1(2 * i + r, r)
                    close1(2 * i + r)
            turn(UNITS - 1)
            dense(UNITS - 1)


def kernel(x, adj, L1_gnn_W, L1_gnn_b):
    import numpy as np
    import concourse.bacc as bacc
    from concourse.bass_utils import run_bass_kernel_spmd

    P, CHUNKS = 128, 4
    x, adj = np.asarray(x), np.asarray(adj)
    n, d = x.shape
    kt = n // P
    adj_t = np.ascontiguousarray(
        adj.reshape(n // P, P, CHUNKS, kt // CHUNKS, P).transpose(0, 2, 4, 3, 1)
    ).reshape(n // P, CHUNKS, P, kt // CHUNKS * P)
    arrays = {"x_dram": x, "adj_dram": adj_t, "w_dram": np.asarray(L1_gnn_W), "b_dram": np.asarray(L1_gnn_b)}
    nc = bacc.Bacc("TRN2", target_bir_lowering=False, num_devices=1)
    args = [nc.dram_tensor(name, a.shape, mybir.dt.from_np(a.dtype), kind="ExternalInput").ap()
            for name, a in arrays.items()]
    out = nc.dram_tensor("out_dram", (n, d), mybir.dt.float32, kind="ExternalOutput").ap()
    gnn_two_layer_kernel(nc, *args, out)
    r = run_bass_kernel_spmd(nc, [arrays], core_ids=[0])
    return r.results[0]["out_dram"]
```

```python
import concourse.bass as bass
from concourse import mybir
from contextlib import ExitStack


def gnn_two_layer_kernel(
    nc: bass.Bass,
    x: bass.AP,
    adj_t: bass.AP,
    w: bass.AP,
    b: bass.AP,
    out: bass.AP,
):
    fp32, fp16, u32 = mybir.dt.float32, mybir.dt.float16, mybir.dt.uint32
    ALU = mybir.AluOpType
    ACT = mybir.ActivationFunctionType
    AX = mybir.AxisListType

    P = 128
    N, D = x.shape
    UNITS = N // P
    KT = N // P
    CHUNKS = 4
    SUBS = 8
    KPC, KPS = KT // CHUNKS, KT // SUBS
    CW, SW = KPC * P, KPS * P
    RAW = 2 * CHUNKS
    RING = 4
    MASKED = (0, 2, 4, 6)
    ADDED = tuple(s for s in range(SUBS) if s not in MASKED)
    NA = len(ADDED)
    AHEAD = SUBS + 2
    COUNT = AHEAD + 3
    GX = KT // SUBS
    HS = 2048.0
    LN_EPS, NORM_EPS = 1e-5, 1e-12
    ONE = 2 * D
    HALF = UNITS // 2

    x_tiles = x.rearrange("(t p) d -> t p d", p=P)
    x_groups = x.rearrange("(g t p) d -> g p t d", p=P, t=GX)
    adj_rows = adj_t.rearrange("u c p f -> (u c p) f")
    x1_dram = nc.dram_tensor("x1_dram", [N, D], fp32, kind="Internal").ap()
    g_dram = nc.dram_tensor("g_dram", [N, 2 * D], fp16, kind="Internal").ap()
    g_chunks = g_dram.rearrange("(c t p) d -> c p t d", p=P, t=KPC)

    ctx = ExitStack()
    with ctx:
        def sb(name, shape, dt):
            return ctx.enter_context(nc.sbuf_tensor(name, shape, dt))

        def pb(name):
            return ctx.enter_context(nc.psum_tensor(name, [P, 512], fp32))

        def sem(name):
            return ctx.enter_context(nc.semaphore(name))

        H = sb("H", [P, KT, 2 * D + 2], fp16)
        raw = sb("raw", [P, RAW, CW], fp32)
        a_hi = sb("a_hi", [P, RING, SW], fp16)
        a_lo = sb("a_lo", [P, RING, SW], fp16)
        pos_keep = sb("pos_keep", [P, 2, len(MASKED), SW], fp16)
        pos_tmp = sb("pos_tmp", [P, SW], fp16)
        nz_tmp = sb("nz_tmp", [P, 2, SW], fp16)
        abs_tmp = sb("abs_tmp", [P, SW], fp32)
        inc = sb("inc", [P, SW], fp32)
        r_row = sb("r_row", [P, 2, P], fp32)
        asum = sb("asum", [P, 2, SUBS + 1], fp32)
        amax = sb("amax", [P, 2, SUBS + 1], fp32)
        am = sb("am", [P, 1], fp32)
        am1 = sb("am1", [P, 1], fp32)
        ebits = sb("ebits", [P, 1], u32)
        scale = sb("scale", [P, UNITS], fp32)
        sc_now = sb("sc_now", [P, 2], fp32)
        un_now = sb("un_now", [P, 2], fp32)
        stats = sb("stats", [P, GX, 6], fp32)
        mv = sb("mv", [P, GX, 2], fp32)
        nt = sb("nt", [P, GX], fp32)
        sd = sb("sd", [P, GX], fp32)
        nw = sb("nw", [P, GX], fp32)
        rs = sb("rs", [P, 2, GX], fp32)
        nb = sb("nb", [P, 2, GX], fp32)
        cnt = sb("cnt", [P, 2], fp32)
        cnt_sq = sb("cnt_sq", [P, 2], fp32)
        cnt_r0 = sb("cnt_r0", [P, 2], fp32)
        cnt_n = sb("cnt_n", [P, 2], fp32)
        cnt_r = sb("cnt_r", [P, 2, 2], fp32)
        diag = sb("diag", [P, P], fp32)
        deg_r = sb("deg_r", [P, 1], fp32)
        agg_t = sb("agg_t", [P, UNITS], fp32)
        self_t = sb("self_t", [P, UNITS], fp32)
        mean_t = sb("mean_t", [P, UNITS], fp32)
        rstd_t = sb("rstd_t", [P, UNITS], fp32)
        rden = sb("rden", [P, 1], fp32)
        st1 = sb("st1", [P, 6], fp32)
        mark = sb("mark", [P, 1], fp32)
        mv1 = sb("mv1", [P, 2], fp32)
        ve = sb("ve", [P, 1], fp32)
        ve_s = sb("ve_s", [P, 1], fp32)
        ve_r = sb("ve_r", [P, 1], fp32)
        ve_n = sb("ve_n", [P, 1], fp32)
        rs_g = sb("rs_g", [P, 1], fp32)
        unit_row = sb("unit_row", [P, 2, 2], fp16)
        ones_f = sb("ones_f", [P, P], fp32)
        ident = sb("ident", [P, P], fp32)

        xz = sb("xz", [P, max(3 * GX, 20) * D], fp32)
        xg = xz[:, 0:2 * GX * D].rearrange("p (b t d) -> p b t d", b=2, d=D)
        zt = xz[:, 2 * GX * D:3 * GX * D].rearrange("p (t d) -> p t d", d=D)
        taken = [0]

        def take(words):
            taken[0] += words
            return xz[:, taken[0] - words:taken[0]]

        x_in = take(2 * D).rearrange("p (b d) -> p b d", b=2)
        x1_o = take(2 * D).rearrange("p (b d) -> p b d", b=2)
        g_o = take(2 * D).bitcast(fp16).rearrange("p (b d) -> p b d", b=2)
        agg = take(D + 2)
        num = take(D + 2)
        z1 = take(D)
        hc = take(D)
        pooled = take(D)
        pooled_t = take(D)
        y = take(D)
        w_sb = take(D // P * D).rearrange("p (c d) -> p c d", d=D)
        b_sb = take(D)

        ps_a = [pb("ps_a0"), pb("ps_a1")]
        ps_m = [pb("ps_m0"), pb("ps_m1")]
        ps_c = [pb("ps_c0"), pb("ps_c1")]
        ps_r = pb("ps_r")
        ps_t, ps_o = ps_m

        raw_in = [sem(f"raw_in{i}") for i in range(RAW)]
        xg_in = [sem("xg_in0"), sem("xg_in1")]
        x_in_got = [sem("x_in_got0"), sem("x_in_got1")]
        x1_st = [sem("x1_st0"), sem("x1_st1")]
        g_st = [sem("g_st0"), sem("g_st1")]
        g_in = [sem(f"g_in{i}") for i in range(CHUNKS)]
        w_in = sem("w_in")
        ident0 = sem("ident0")
        const_set = sem("const_set")
        ones_h = sem("ones_h")
        ln_step = sem("ln_step")
        ln_var = sem("ln_var")
        ln_sd = sem("ln_sd")
        ln_rs = sem("ln_rs")
        z_done = sem("z_done")
        h_hi = sem("h_hi")
        h_done = sem("h_done")
        abs_done = sem("abs_done")
        nz_done = sem("nz_done")
        pos_done = sem("pos_done")
        counted = sem("counted")
        amax_done = sem("amax_done")
        sc_step = sem("sc_step")
        scale_done = sem("scale_done")
        cnt_done = sem("cnt_done")
        cnt_root = sem("cnt_root")
        cnt_step = sem("cnt_step")
        diag_done = sem("diag_done")
        r_mat = sem("r_mat")
        r_row_done = sem("r_row_done")
        half_done = sem("half_done")
        inc_done = sem("inc_done")
        hi_done = sem("hi_done")
        lo_done = sem("lo_done")
        sub_done = sem("sub_done")
        agg_done = sem("agg_done")
        num_done = sem("num_done")
        ep_step = sem("ep_step")
        x1_done = sem("x1_done")
        ve_done = sem("ve_done")
        ve_root = sem("ve_root")
        g_done = sem("g_done")
        own1 = sem("own1")
        pool_done = sem("pool_done")
        tp_done = sem("tp_done")
        tc_done = sem("tc_done")
        o_done = sem("o_done")
        y_done = sem("y_done")
        res_done = sem("res_done")

        block = ctx.enter_context(nc.Block())

        def is_zero(v):
            return isinstance(v, int) and v == 0

        def sub_at(par, s):
            return raw[:, CHUNKS * par + s // 2, (s % 2) * SW:(s % 2 + 1) * SW]

        def pos_at(par, s):
            return pos_keep[:, par, MASKED.index(s), :] if s in MASKED else pos_tmp[:, :]

        def fills(u, par):
            return (u - par) // 2 + 1 if isinstance(u, int) else u

        @block.sync
        def _(sp):
            def load_chunk(v, j, src_unit, par, first=False):
                if not first:
                    sp.wait_ge(lo_done, SUBS * (v - 2) + 2 * j + 2)
                row = (src_unit * CHUNKS + j) * P
                sp.dma_start(raw[:, CHUNKS * par + j, :], adj_rows[bass.ds(row, P), :])\
                    .then_inc(raw_in[CHUNKS * par + j], 16)

            def load_xg(g):
                if g >= 2:
                    sp.wait_ge(z_done, GX * (g - 1))
                sp.dma_start(xg[:, g % 2, :, :], x_groups[g]).then_inc(xg_in[g % 2], 16)

            load_xg(0)
            for j in range(CHUNKS):
                load_chunk(0, j, 0, 0, first=True)
            load_xg(1)
            for j in range(CHUNKS):
                load_chunk(1, j, 1, 1, first=True)
            for g in range(2, SUBS):
                load_xg(g)

            def store0(u, par):
                sp.wait_ge(x1_done, u + 1)
                sp.dma_start(x1_dram[bass.ds(u * P, P), :], x1_o[:, par, :]).then_inc(x1_st[par], 16)
                sp.wait_ge(g_done, u + 1)
                sp.dma_start(g_dram[bass.ds(u * P, P), :], g_o[:, par, :]).then_inc(g_st[par], 16)

            def step0(u, par, first=False, wrap=False, last=False):
                for j in range(CHUNKS):
                    load_chunk(u + 2, j, u + 2 - UNITS if wrap else u + 2, par)
                if first:
                    sp.wait_ge(h_done, KT)
                    sp.dma_start(x_in[:, 0, :], x_tiles[0]).then_inc(x_in_got[0], 16)
                    sp.dma_start(w_sb[:, :, :], w.rearrange("(c p) n -> p c n", p=P)).then_inc(w_in, 16)
                    sp.dma_start(b_sb[:, :], b.partition_broadcast(P)).then_inc(w_in, 16)
                else:
                    store0(u - 1, 1 - par)
                if not last:
                    sp.dma_start(x_in[:, 1 - par, :], x[bass.ds((u + 1) * P, P), :])\
                        .then_inc(x_in_got[1 - par], 16)

            step0(0, 0, first=True)
            with nc.sync.Fori(0, HALF - 2) as i:
                step0(2 * i + 1, 1)
                step0(2 * i + 2, 0)
            step0(UNITS - 3, 1)
            step0(UNITS - 2, 0, wrap=True)
            step0(UNITS - 1, 1, wrap=True, last=True)

            for c in range(CHUNKS):
                if c == CHUNKS - 1:
                    store0(UNITS - 1, 1)
                sp.wait_ge(sub_done, SUBS * (UNITS - 1) + 2 * c + 2)
                for par in range(2):
                    sp.wait_ge(g_st[par], 16 * (KPC * (c + 1) // 2))
                sp.dma_start(H[:, c * KPC:(c + 1) * KPC, 0:2 * D], g_chunks[c]).then_inc(g_in[c], 16)
            for par in range(2):
                sp.wait_ge(x1_st[par], 16 * HALF)
                sp.dma_start(x_in[:, par, :], x1_dram[par * P:(par + 1) * P, :]).then_inc(x_in_got[par], 16)

            def store1(u, par):
                sp.wait_ge(res_done, u + 1)
                sp.dma_start(out[bass.ds(u * P, P), :], x1_o[:, par, :]).then_inc(x1_st[par], 16)

            def step1(u, par, first=False, more=True, last=False):
                if more:
                    for j in range(CHUNKS):
                        load_chunk(UNITS + u + 2, j, u + 2, par)
                if not first:
                    store1(u - 1, 1 - par)
                    if not last:
                        sp.dma_start(x_in[:, 1 - par, :], x1_dram[bass.ds((u + 1) * P, P), :])\
                            .then_inc(x_in_got[1 - par], 16)

            step1(0, 0, first=True)
            with nc.sync.Fori(0, HALF - 2) as i:
                step1(2 * i + 1, 1)
                step1(2 * i + 2, 0)
            step1(UNITS - 3, 1)
            step1(UNITS - 2, 0, more=False)
            step1(UNITS - 1, 1, more=False, last=True)
            store1(UNITS - 1, 1)
            for par in range(2):
                sp.wait_ge(x1_st[par], 16 * UNITS)
                sp.wait_ge(g_st[par], 16 * HALF)

        @block.gpsimd
        def _(pool):
            nc.gpsimd.memset(ident[:, :], 0.0).then_inc(ident0, 1)
            nc.gpsimd.memset(asum[:, :, SUBS:SUBS + 1], 1.0).then_inc(ident0, 1)
            nc.gpsimd.memset(unit_row[:, :, :], 0.0).then_inc(ident0, 1)
            nc.gpsimd.memset(ones_f[:, :], 1.0).then_inc(const_set, 1)
            nc.gpsimd.memset(H[:, :, ONE:ONE + 1], HS).then_inc(ones_h, 1)
            pool.wait_ge(ident0, 3)
            nc.gpsimd.memset(unit_row[:, 0, 0:1], 1.0).then_inc(const_set, 1)
            nc.gpsimd.memset(unit_row[:, 1, 1:2], 1.0).then_inc(const_set, 1)
            nc.gpsimd.affine_select(out=ident[:, :], in_=ident[:, :], compare_op=ALU.not_equal, fill=1.0,
                                    base=0, pattern=[[-1, P]], channel_multiplier=1).then_inc(const_set, 1)
            for u in range(UNITS):
                pool.wait_ge(abs_done, SUBS * (u + 1))
                nc.gpsimd.partition_all_reduce(amax[:, u % 2, :], asum[:, u % 2, :], P,
                                               bass.bass_isa.ReduceOp.max).then_inc(amax_done, 1)

        @block.scalar
        def _(act):
            def look(m, par, s, uses, first=False):
                if s % 2 == 0:
                    act.wait_ge(raw_in[CHUNKS * par + s // 2], 16 * uses)
                if not is_zero(m):
                    act.wait_ge(nz_done, m)
                nc.scalar.activation(abs_tmp[:, :], sub_at(par, s), ACT.Abs,
                                     accum_out=asum[:, par, s:s + 1]).then_inc(abs_done, 1)
                act.wait_ge(abs_done, m + 1)
                if not first:
                    act.wait_ge(counted, m - 1)
                nc.scalar.activation(nz_tmp[:, s % 2, :], abs_tmp[:, :], ACT.Sign).then_inc(nz_done, 1)

            def split_hi(v, par, s, src, free=True):
                if free:
                    act.wait_ge(sub_done, SUBS * v + s - RING + 1)
                nc.scalar.activation(a_hi[:, s % RING, :], src, ACT.Copy,
                                     scale=sc_now[:, par:par + 1]).then_inc(hi_done, 1)

            def roots(u):
                act.wait_ge(cnt_done, u + 1)
                nc.scalar.activation(cnt_sq[:, :], cnt[:, :], ACT.Sqrt).then_inc(cnt_root, 1)

            def ln_root(g):
                act.wait_ge(ln_var, g + 1)
                nc.scalar.activation(sd[:, :], nt[:, :], ACT.Sqrt).then_inc(ln_sd, 1)

            def features(g, t0, t1):
                act.wait_ge(ln_rs, 2 * (g + 1))
                for t in range(t0, t1 + 1):
                    n = g * GX + t
                    if t < t1:
                        if n >= GX:
                            act.wait_ge(h_done, n - GX + 1)
                        nc.scalar.activation(zt[:, t, :], xg[:, g % 2, t, :], ACT.Identity,
                                             bias=nb[:, g % 2, t:t + 1], scale=rs[:, g % 2, t:t + 1])\
                            .then_inc(z_done, 1)
                    if t > t0:
                        act.wait_ge(z_done, n)
                        nc.scalar.activation(H[:, n - 1, D:2 * D], zt[:, t - 1, :], ACT.Relu).then_inc(h_hi, 1)

            def epilogue0(u, par):
                act.wait_ge(sub_done, SUBS * (u + 1))
                if not is_zero(u):
                    act.wait_ge(num_done, u)
                nc.scalar.activation(agg[:, 0:D + 1], ps_a[par][:, 0:D + 1], ACT.Copy,
                                     scale=un_now[:, par:par + 1]).then_inc(agg_done, 1)

            def ve_roots(u):
                act.wait_ge(ve_done, u + 1)
                nc.scalar.activation(ve_s[:, :], ve[:, :], ACT.Sqrt).then_inc(ve_root, 1)

            def step0(u, par, half, first=False, ahead=SUBS):
                for s in range(SUBS):
                    if first:
                        mid = (GX + 1) // 2
                        features(s, 0, mid)
                        if s < SUBS - 1:
                            ln_root(s + 1)
                        if mid < GX:
                            features(s, mid, GX)
                    if s < ahead:
                        over = (s + AHEAD) // SUBS
                        look(SUBS * u + s + AHEAD, (par + over) % 2, (s + AHEAD) % SUBS,
                             half + (par + over) // 2 + 1)
                    if s == 5 and not first:
                        ve_roots(u - 1)
                    if s == 6 and ahead:
                        roots(u + 1)
                    if s == 0:
                        act.wait_ge(scale_done, u + 1)
                    if s in ADDED:
                        act.wait_ge(inc_done, NA * u + ADDED.index(s) + 1)
                        src = inc[:, :]
                    else:
                        src = sub_at(par, s)
                    split_hi(u, par, s, src, free=not (first and s < RING))
                    if s == 0:
                        act.wait_ge(r_mat, u + 1)
                        nc.scalar.activation(r_row[:, par, :], ps_r[:, 0:P], ACT.Copy).then_inc(r_row_done, 1)
                    if s == RING - 1 and not first:
                        epilogue0(u - 1, 1 - par)

            for m in range(AHEAD):
                look(m, m // SUBS, m % SUBS, 1, first=m < 2)
            roots(0)
            ln_root(0)
            step0(0, 0, 0, first=True)
            step0(1, 1, 0)
            step0(2, 0, 1)
            with nc.scalar.Fori(1, HALF - 2) as i:
                step0(2 * i + 1, 1, i)
                step0(2 * i + 2, 0, i + 1)
            step0(UNITS - 3, 1, HALF - 2)
            step0(UNITS - 2, 0, HALF - 1, ahead=2 * SUBS - AHEAD)
            step0(UNITS - 1, 1, HALF - 1, ahead=0)

            def turn(u):
                act.wait_ge(tp_done, u + 1)
                if not is_zero(u):
                    act.wait_ge(o_done, u)
                nc.scalar.activation(pooled_t[:, :], ps_t[:, 0:D], ACT.Copy).then_inc(tc_done, 1)

            def step1(u, par, uses, first=False):
                act.wait_ge(scale_done, UNITS + u + 1)
                for s in range(SUBS):
                    if s % 2 == 0:
                        act.wait_ge(raw_in[CHUNKS * par + s // 2], 16 * uses)
                    split_hi(UNITS + u, par, s, sub_at(par, s))
                    if s == RING - 1 and first:
                        epilogue0(UNITS - 1, 1)
                        ve_roots(UNITS - 1)
                    if s == SUBS - 2 and not first:
                        turn(u - 1)

            step1(0, 0, HALF + 1, first=True)
            step1(1, 1, HALF + 1)
            step1(2, 0, HALF + 2)
            with nc.scalar.Fori(1, HALF - 1) as i:
                step1(2 * i + 1, 1, HALF + i + 1)
                step1(2 * i + 2, 0, HALF + i + 2)
            step1(UNITS - 1, 1, UNITS)
            turn(UNITS - 1)

        @block.vector
        def _(dve):
            def link(ins, step_sem, count):
                ins.then_inc(step_sem, 1)
                dve.wait_ge(step_sem, count)

            def ln_stats(g):
                dve.wait_ge(xg_in[g % 2], 16 * (g // 2 + 1))
                for t in range(GX):
                    last = nc.vector.bn_stats(stats[:, t, :], xg[:, g % 2, t, :])
                link(last, ln_step, 6 * g + 1)
                for t in range(GX):
                    last = nc.vector.bn_aggr(mv[:, t, :], stats[:, t, :])
                link(last, ln_step, 6 * g + 2)
                nc.vector.tensor_scalar(nt[:, :], mv[:, :, 1], LN_EPS, None, ALU.add).then_inc(ln_var, 1)

            def ln_factors(g, part):
                r, n = rs[:, g % 2, :], nw[:, :]
                base = 6 * g + 2
                if part == 0:
                    dve.wait_ge(ln_sd, g + 1)
                    nc.vector.reciprocal(r, sd[:, :]).then_inc(ln_step, 1)
                if part == 1:
                    dve.wait_ge(ln_step, base + 1)
                    nc.vector.tensor_tensor(n, nt[:, :], r, ALU.mult).then_inc(ln_step, 1)
                if part == 2:
                    dve.wait_ge(ln_step, base + 2)
                    nc.vector.tensor_tensor(n, n, r, ALU.mult).then_inc(ln_step, 1)
                if part == 3:
                    dve.wait_ge(ln_step, base + 3)
                    nc.vector.tensor_scalar(n, n, -0.5 * HS, 1.5 * HS, ALU.mult, ALU.add).then_inc(ln_step, 1)
                if part == 4:
                    dve.wait_ge(ln_step, base + 4)
                    nc.vector.tensor_tensor(r, r, n, ALU.mult).then_inc(ln_rs, 1)
                if part == 5:
                    dve.wait_ge(ln_rs, 2 * g + 1)
                    nc.vector.scalar_tensor_tensor(out=nb[:, g % 2, :], in0=mv[:, :, 0], scalar=-1.0, in1=r,
                                                   op0=ALU.mult, op1=ALU.mult).then_inc(ln_rs, 1)

            def features_lo(g):
                for t in range(max(GX, 6)):
                    if t < GX:
                        n = g * GX + t
                        dve.wait_ge(h_hi, n + 1)
                        nc.vector.scalar_tensor_tensor(out=H[:, n, 0:D], in0=zt[:, t, :], scalar=0.0,
                                                       in1=H[:, n, D:2 * D], op0=ALU.max, op1=ALU.subtract)\
                            .then_inc(h_done, 1)
                    if t < 6 and g < SUBS - 1:
                        ln_factors(g + 1, t)

            def mask(m, par, s, uses, first=False):
                if s % 2 == 0:
                    dve.wait_ge(raw_in[CHUNKS * par + s // 2], 16 * uses)
                if s in ADDED and not first:
                    dve.wait_ge(counted, m - 1)
                nc.vector.tensor_scalar(pos_at(par, s), sub_at(par, s), 0.0, None, ALU.is_gt)\
                    .then_inc(pos_done, 1)

            def find_scale(u, par, part):
                base = 2 * u
                if part == 0:
                    dve.wait_ge(amax_done, u + 1)
                    nc.vector.reduce_max(am[:, :], amax[:, par, :], AX.X).then_inc(sc_step, 1)
                if part == 1:
                    dve.wait_ge(sc_step, base + 1)
                    nc.vector.tensor_scalar(ebits[:, :], am[:, :].bitcast(u32), 0x7F800000, None,
                                            ALU.bitwise_and).then_inc(sc_step, 1)
                if part == 2:
                    dve.wait_ge(sc_step, base + 2)
                    nc.vector.tensor_scalar(un_now[:, par:par + 1].bitcast(u32), ebits[:, :],
                                            -float(13 << 23), None, ALU.add)
                    nc.vector.tensor_scalar(sc_now[:, par:par + 1].bitcast(u32), ebits[:, :], -1.0,
                                            float(267 << 23), ALU.mult, ALU.add).then_inc(scale_done, 1)

            def take_counts(u, par):
                dve.wait_ge(counted, SUBS * (u + 1))
                nc.vector.tensor_copy(cnt[:, 0:1], ps_c[par][:, 0:1])
                nc.vector.tensor_scalar(cnt[:, 1:2], ps_c[par][:, 1:2], 1.0, None, ALU.max)\
                    .then_inc(cnt_done, 1)

            def find_rows(u, par, part):
                base = 7 * u
                r0, n, r = cnt_r0[:, :], cnt_n[:, :], cnt_r[:, par, :]
                if part == 0:
                    dve.wait_ge(cnt_root, u + 1)
                    nc.vector.tensor_scalar(n, cnt_sq[:, :], NORM_EPS, None, ALU.max).then_inc(cnt_step, 1)
                if part == 1:
                    dve.wait_ge(cnt_step, base + 1)
                    nc.vector.reciprocal(r0, n).then_inc(cnt_step, 1)
                if part == 2:
                    dve.wait_ge(cnt_step, base + 2)
                    dve.wait_ge(cnt_done, u + 1)
                    for c in range(2):
                        nc.vector.scalar_tensor_tensor(out=n[:, c:c + 1], in0=r0[:, c:c + 1],
                                                       scalar=cnt[:, c:c + 1], in1=r0[:, c:c + 1],
                                                       op0=ALU.mult, op1=ALU.mult).then_inc(cnt_step, 1)
                if part == 3:
                    dve.wait_ge(cnt_step, base + 4)
                    nc.vector.tensor_scalar(n, n, -0.5, 1.5, ALU.mult, ALU.add).then_inc(cnt_step, 1)
                if part == 4:
                    dve.wait_ge(cnt_step, base + 5)
                    nc.vector.tensor_tensor(r, r0, n, ALU.mult).then_inc(cnt_step, 1)
                if part == 5:
                    dve.wait_ge(cnt_step, base + 6)
                    nc.vector.tensor_scalar(diag[:, :], ident[:, :], r[:, 0:1], None, ALU.mult)\
                        .then_inc(diag_done, 1)
                    nc.vector.tensor_scalar(deg_r[:, :], r[:, 1:2], r[:, 1:2], None, ALU.mult)\
                        .then_inc(cnt_step, 1)
                if part == 6:
                    dve.wait_ge(cnt_step, base + 7)
                    dve.wait_ge(scale_done, u + 1)
                    nc.vector.tensor_copy(scale[:, bass.ds(u, 1)], sc_now[:, par:par + 1])
                    nc.vector.tensor_scalar(self_t[:, bass.ds(u, 1)], deg_r[:, :], 1.0, None, ALU.add)
                    nc.vector.scalar_tensor_tensor(out=agg_t[:, bass.ds(u, 1)], in0=deg_r[:, :],
                                                   scalar=1.0 / HS, in1=un_now[:, par:par + 1],
                                                   op0=ALU.mult, op1=ALU.mult)

            def split_lo(v, par, s, src):
                dve.wait_ge(hi_done, SUBS * v + s + 1)
                nc.vector.scalar_tensor_tensor(out=a_lo[:, s % RING, :], in0=src,
                                               scalar=sc_now[:, par:par + 1], in1=a_hi[:, s % RING, :],
                                               op0=ALU.mult, op1=ALU.subtract).then_inc(lo_done, 1)

            def split_lo0(u, par, s):
                split_lo(u, par, s, inc[:, :] if s in ADDED else sub_at(par, s))

            EP = 9

            def epilogue0(u, par, uses, part):
                base = EP * u
                again = not (isinstance(uses, int) and uses == 1)
                x1 = x1_o[:, par, :]
                if part == 0:
                    dve.wait_ge(sub_done, SUBS * (u + 1))
                    dve.wait_ge(agg_done, u + 1)
                    nc.vector.scalar_tensor_tensor(out=num[:, 0:D + 1], in0=ps_m[par][:, 0:D + 1],
                                                   scalar=cnt_r[:, par, 0:1], in1=agg[:, 0:D + 1],
                                                   op0=ALU.mult, op1=ALU.add).then_inc(num_done, 1)
                if part == 1:
                    dve.wait_ge(num_done, u + 1)
                    nc.vector.reciprocal(rden[:, :], num[:, D:D + 1]).then_inc(ep_step, 1)
                if part == 2:
                    dve.wait_ge(ep_step, base + 1)
                    dve.wait_ge(x_in_got[par], 16 * uses)
                    if again:
                        dve.wait_ge(x1_st[par], 16 * (uses - 1))
                    nc.vector.scalar_tensor_tensor(out=x1, in0=num[:, 0:D], scalar=rden[:, :],
                                                   in1=x_in[:, par, :], op0=ALU.mult, op1=ALU.add)\
                        .then_inc(x1_done, 1)
                if part == 3:
                    dve.wait_ge(x1_done, u + 1)
                    nc.vector.bn_stats(st1[:, :], x1).then_inc(ep_step, 1)
                if part == 4:
                    dve.wait_ge(ep_step, base + 2)
                    nc.vector.tensor_copy(mark[:, :], rden[:, :])
                    nc.vector.bn_aggr(mv1[:, :], st1[:, :]).then_inc(ep_step, 1)
                if part == 5:
                    dve.wait_ge(ep_step, base + 3)
                    nc.vector.tensor_scalar(ve[:, :], mv1[:, 1:2], LN_EPS, None, ALU.add).then_inc(ve_done, 1)
                    nc.vector.tensor_copy(mean_t[:, bass.ds(u, 1)], mv1[:, 0:1])
                if part == 6:
                    dve.wait_ge(ve_root, u + 1)
                    nc.vector.reciprocal(ve_r[:, :], ve_s[:, :]).then_inc(ep_step, 1)
                if part == 7:
                    dve.wait_ge(ep_step, base + 4)
                    nc.vector.scalar_tensor_tensor(out=ve_n[:, :], in0=ve[:, :], scalar=ve_r[:, :],
                                                   in1=ve_r[:, :], op0=ALU.mult, op1=ALU.mult)\
                        .then_inc(ep_step, 1)
                if part == 8:
                    dve.wait_ge(ep_step, base + 5)
                    nc.vector.tensor_scalar(ve_n[:, :], ve_n[:, :], -0.5, 1.5, ALU.mult, ALU.add)\
                        .then_inc(ep_step, 1)
                if part == 9:
                    dve.wait_ge(ep_step, base + 6)
                    nc.vector.tensor_tensor(rstd_t[:, bass.ds(u, 1)], ve_r[:, :], ve_n[:, :], ALU.mult)
                    nc.vector.scalar_tensor_tensor(out=rs_g[:, :], in0=ve_r[:, :], scalar=HS, in1=ve_n[:, :],
                                                   op0=ALU.mult, op1=ALU.mult).then_inc(ep_step, 1)
                if part == 10:
                    dve.wait_ge(ep_step, base + 7)
                    nc.vector.tensor_scalar(z1, x1, mv1[:, 0:1], rs_g[:, :], ALU.subtract, ALU.mult)\
                        .then_inc(ep_step, 1)
                if part == 11:
                    dve.wait_ge(ep_step, base + 8)
                    if again:
                        dve.wait_ge(g_st[par], 16 * (uses - 1))
                    nc.vector.tensor_scalar(g_o[:, par, D:2 * D], z1, 0.0, None, ALU.max)\
                        .then_inc(ep_step, 1)
                if part == 12:
                    dve.wait_ge(ep_step, base + 9)
                    nc.vector.scalar_tensor_tensor(out=g_o[:, par, 0:D], in0=z1, scalar=0.0,
                                                   in1=g_o[:, par, D:2 * D], op0=ALU.max, op1=ALU.subtract)\
                        .then_inc(g_done, 1)

            EPILOGUE_AT = {(3, 3): 0, (4, 1): 1, (4, 3): 2, (5, 0): 3, (5, 1): 4, (5, 2): 5, (6, 1): 6,
                           (6, 3): 7, (7, 0): 8, (7, 1): 9, (7, 2): 10, (7, 3): 11}
            SCALE_AT = {(6, 3): 0, (7, 0): 1, (7, 1): 2}
            ROWS_AT = {(7, 0): 0, (7, 1): 1, (7, 2): 2, (7, 3): 3}
            ROWS_THEN = {(0, 1): 4, (0, 3): 5, (1, 0): 6}

            def step0(u, par, half, first=False, ahead=SUBS):
                def between(s, place):
                    if (s, place) in EPILOGUE_AT and not first:
                        epilogue0(u - 1, 1 - par, half + par, EPILOGUE_AT[s, place])
                        if EPILOGUE_AT[s, place] == 11:
                            epilogue0(u - 1, 1 - par, half + par, 12)
                    if (s, place) == (6, 1) and ahead:
                        take_counts(u + 1, 1 - par)
                    if (s, place) in SCALE_AT and ahead:
                        find_scale(u + 1, 1 - par, SCALE_AT[s, place])
                    if (s, place) in ROWS_AT and ahead:
                        find_rows(u + 1, 1 - par, ROWS_AT[s, place])
                    if (s, place) in ROWS_THEN and not first:
                        find_rows(u, par, ROWS_THEN[s, place])

                for s in range(SUBS):
                    n = SUBS * u + s
                    if first:
                        if s < SUBS - 1:
                            ln_stats(s + 1)
                        features_lo(s)
                    if s == ADDED[0]:
                        dve.wait_ge(r_row_done, u + 1)
                    if s in ADDED:
                        nth = NA * u + ADDED.index(s) + 1
                        if not (first and s < 3):
                            dve.wait_ge(hi_done, n - 1)
                            dve.wait_ge(lo_done, n - 1)
                        nc.vector.scalar_tensor_tensor(
                            out=inc[:, :].rearrange("p (k r) -> p k r", r=P),
                            in0=sub_at(par, s).rearrange("p (k r) -> p k r", r=P), scalar=0.0,
                            in1=r_row[:, par:par + 1, :].to_broadcast([P, KPS, P]),
                            op0=ALU.is_gt, op1=ALU.mult).then_inc(half_done, 1)
                        between(s, 0)
                    if s < ahead:
                        over = (s + AHEAD) // SUBS
                        mask(n + AHEAD, (par + over) % 2, (s + AHEAD) % SUBS, half + (par + over) // 2 + 1)
                    between(s, 1)
                    if s in ADDED:
                        dve.wait_ge(half_done, nth)
                        nc.vector.tensor_tensor(inc[:, :], inc[:, :], sub_at(par, s),
                                                ALU.add).then_inc(inc_done, 1)
                        between(s, 2)
                    if s > 0:
                        split_lo0(u, par, s - 1)
                    elif not first:
                        split_lo0(u - 1, 1 - par, SUBS - 1)
                    between(s, 3)

            for m in range(AHEAD):
                mask(m, m // SUBS, m % SUBS, 1, first=m < 2)
            dve.wait_ge(const_set, 4)
            take_counts(0, 0)
            for part in range(3):
                find_scale(0, 0, part)
            for part in range(7):
                find_rows(0, 0, part)
            ln_stats(0)
            for part in range(6):
                ln_factors(0, part)
            step0(0, 0, 0, first=True)
            step0(1, 1, 0)
            step0(2, 0, 1)
            with nc.vector.Fori(1, HALF - 2) as i:
                step0(2 * i + 1, 1, i)
                step0(2 * i + 2, 0, i + 1)
            step0(UNITS - 3, 1, HALF - 2)
            step0(UNITS - 2, 0, HALF - 1, ahead=2 * SUBS - AHEAD)
            step0(UNITS - 1, 1, HALF - 1, ahead=0)
            split_lo0(UNITS - 1, 1, SUBS - 1)

            def pool_row(u, par, uses):
                base = 2 * u
                dve.wait_ge(x_in_got[par], 16 * uses)
                link(nc.vector.tensor_scalar(z1, x_in[:, par, :], mean_t[:, bass.ds(u, 1)],
                                             rstd_t[:, bass.ds(u, 1)], ALU.subtract, ALU.mult), own1, base + 1)
                link(nc.vector.tensor_scalar(hc, z1, 0.0, self_t[:, bass.ds(u, 1)], ALU.max, ALU.mult),
                     own1, base + 2)
                dve.wait_ge(sub_done, SUBS * (UNITS + u + 1))
                if not is_zero(u):
                    dve.wait_ge(tp_done, u)
                nc.vector.scalar_tensor_tensor(out=pooled, in0=ps_a[par][:, 0:D],
                                               scalar=agg_t[:, bass.ds(u, 1)], in1=hc,
                                               op0=ALU.mult, op1=ALU.add).then_inc(pool_done, 1)

            def result(u, par, uses):
                dve.wait_ge(o_done, u + 1)
                link(nc.vector.tensor_tensor(y, ps_o[:, 0:D], b_sb, ALU.add), y_done, u + 1)
                dve.wait_ge(x1_st[par], 16 * (uses - 1))
                nc.vector.scalar_tensor_tensor(out=x1_o[:, par, :], in0=y, scalar=0.0, in1=x_in[:, par, :],
                                               op0=ALU.max, op1=ALU.add).then_inc(res_done, 1)

            def step1(u, par, uses, before=None):
                if before is not None:
                    dve.wait_ge(hi_done, SUBS * (UNITS + u - 1))
                link(nc.vector.tensor_copy(sc_now[:, par:par + 1], scale[:, bass.ds(u, 1)]),
                     scale_done, UNITS + u + 1)
                for s in range(SUBS):
                    if s % 2 == 0:
                        dve.wait_ge(raw_in[CHUNKS * par + s // 2], 16 * uses)
                    split_lo(UNITS + u, par, s, sub_at(par, s))
                    if s == RING - 1 and before is None:
                        for part in range(13):
                            epilogue0(UNITS - 1, 1, HALF, part)
                    elif s == RING - 1:
                        pool_row(u - 1, 1 - par, before)
                    if s == SUBS - 2 and before is not None:
                        result(u - 1, 1 - par, before)

            dve.wait_ge(w_in, 32)
            step1(0, 0, HALF + 1)
            step1(1, 1, HALF + 1, HALF + 1)
            step1(2, 0, HALF + 2, HALF + 1)
            with nc.vector.Fori(1, HALF - 1) as i:
                step1(2 * i + 1, 1, HALF + i + 1, HALF + i + 1)
                step1(2 * i + 2, 0, HALF + i + 2, HALF + i + 1)
            step1(UNITS - 1, 1, UNITS, UNITS)
            pool_row(UNITS - 1, 1, UNITS)
            result(UNITS - 1, 1, UNITS)

        @block.tensor
        def _(pe):
            pe.wait_ge(ones_h, 1)
            pe.wait_ge(const_set, 4)

            def count(m, par, s):
                pe.wait_ge(pos_done, m + 1)
                pe.wait_ge(nz_done, m + 1)
                for k in range(KPS):
                    nc.tensor.matmul(ps_c[par][:, 0:2], pos_at(par, s)[:, k * P:(k + 1) * P], unit_row[:, 0, :],
                                     start=(s == 0 and k == 0), stop=False)
                    last = nc.tensor.matmul(ps_c[par][:, 0:2], nz_tmp[:, s % 2, k * P:(k + 1) * P],
                                            unit_row[:, 1, :], start=False,
                                            stop=(s == SUBS - 1 and k == KPS - 1))
                last.then_inc(counted, 1)

            def rows_over(u):
                pe.wait_ge(diag_done, u + 1)
                if not is_zero(u):
                    pe.wait_ge(r_row_done, u)
                nc.tensor.matmul(ps_r[:, 0:P], ones_f[:, :], diag[:, :], start=True, stop=True)\
                    .then_inc(r_mat, 1)

            def unit0(u, par, first=False, free=True, ahead=SUBS):
                if free:
                    pe.wait_ge(agg_done, u - 1)
                    pe.wait_ge(num_done, u - 1)
                PA, PM = ps_a[par], ps_m[par]
                for s in range(SUBS):
                    pe.wait_ge(hi_done, SUBS * u + s + 1)
                    pe.wait_ge(lo_done, SUBS * u + s + 1)
                    for k in range(KPS):
                        kt = s * KPS + k
                        if first:
                            pe.wait_ge(h_done, kt + 1)
                        hi = a_hi[:, s % RING, k * P:(k + 1) * P]
                        lo = a_lo[:, s % RING, k * P:(k + 1) * P]
                        h_hi1, h_lo = H[:, kt, D:2 * D + 1], H[:, kt, 0:D]
                        nc.tensor.matmul(PA[:, 0:D + 1], hi, h_hi1, start=(kt == 0), stop=False)
                        nc.tensor.matmul(PA[:, 0:D], hi, h_lo, start=False, stop=False)
                        last = nc.tensor.matmul(PA[:, 0:D + 1], lo, h_hi1, start=False, stop=(kt == KT - 1))
                        if s in MASKED:
                            pos = pos_at(par, s)[:, k * P:(k + 1) * P]
                            end = kt == (MASKED[-1] + 1) * KPS - 1
                            nc.tensor.matmul(PM[:, 0:D + 1], pos, h_hi1, start=(kt == 0), stop=False)
                            last = nc.tensor.matmul(PM[:, 0:D], pos, h_lo, start=False, stop=end)
                    last.then_inc(sub_done, 1)
                    if s < ahead:
                        over = (s + COUNT) // SUBS
                        count(SUBS * u + s + COUNT, (par + over) % 2, (s + COUNT) % SUBS)
                    if s == 5 and ahead:
                        rows_over(u + 1)

            for m in range(COUNT):
                count(m, m // SUBS, m % SUBS)
                if m == SUBS - 1:
                    rows_over(0)
            unit0(0, 0, first=True, free=False)
            unit0(1, 1, free=False)
            with nc.tensor.Fori(1, HALF - 1) as i:
                unit0(2 * i, 0)
                unit0(2 * i + 1, 1)
            unit0(UNITS - 2, 0, ahead=SUBS * 2 - COUNT)
            unit0(UNITS - 1, 1, ahead=0)

            def turn(u):
                pe.wait_ge(pool_done, u + 1)
                for c in range(D // P):
                    last = nc.tensor.transpose(ps_t[:, c * P:(c + 1) * P], pooled[:, c * P:(c + 1) * P], ident[:, :])
                last.then_inc(tp_done, 1)

            def dense(u):
                pe.wait_ge(tc_done, u + 1)
                if not is_zero(u):
                    pe.wait_ge(y_done, u)
                for c in range(D // P):
                    last = nc.tensor.matmul(ps_o[:, 0:D], pooled_t[:, c * P:(c + 1) * P], w_sb[:, c, :],
                                            start=(c == 0), stop=(c == D // P - 1))
                last.then_inc(o_done, 1)

            def unit1(u, par, first=False, free=True):
                if free:
                    pe.wait_ge(pool_done, u - 1)
                PA = ps_a[par]
                for s in range(SUBS):
                    if first and s % 2 == 0:
                        pe.wait_ge(g_in[s // 2], 16)
                    pe.wait_ge(hi_done, SUBS * (UNITS + u) + s + 1)
                    pe.wait_ge(lo_done, SUBS * (UNITS + u) + s + 1)
                    for k in range(KPS):
                        kt = s * KPS + k
                        hi = a_hi[:, s % RING, k * P:(k + 1) * P]
                        lo = a_lo[:, s % RING, k * P:(k + 1) * P]
                        nc.tensor.matmul(PA[:, 0:D], hi, H[:, kt, D:2 * D], start=(kt == 0), stop=False)
                        nc.tensor.matmul(PA[:, 0:D], hi, H[:, kt, 0:D], start=False, stop=False)
                        last = nc.tensor.matmul(PA[:, 0:D], lo, H[:, kt, D:2 * D], start=False,
                                                stop=(kt == KT - 1))
                    last.then_inc(sub_done, 1)
                    if s == 2 and not first:
                        turn(u - 1)
                    if s == RING and not first:
                        dense(u - 1)

            pe.wait_ge(w_in, 32)
            pe.wait_ge(agg_done, UNITS - 1)
            pe.wait_ge(num_done, UNITS - 1)
            unit1(0, 0, first=True, free=False)
            pe.wait_ge(agg_done, UNITS)
            pe.wait_ge(num_done, UNITS)
            unit1(1, 1, free=False)
            with nc.tensor.Fori(1, HALF) as i:
                unit1(2 * i, 0)
                unit1(2 * i + 1, 1)
            turn(UNITS - 1)
            dense(UNITS - 1)


def kernel(x, adj, L1_gnn_W, L1_gnn_b):
    import numpy as np
    import concourse.bacc as bacc
    from concourse.bass_utils import run_bass_kernel_spmd

    P, CHUNKS = 128, 4
    x, adj = np.asarray(x), np.asarray(adj)
    n, d = x.shape
    kt = n // P
    adj_t = np.ascontiguousarray(
        adj.reshape(n // P, P, CHUNKS, kt // CHUNKS, P).transpose(0, 2, 4, 3, 1)
    ).reshape(n // P, CHUNKS, P, kt // CHUNKS * P)
    arrays = {"x_dram": x, "adj_dram": adj_t, "w_dram": np.asarray(L1_gnn_W), "b_dram": np.asarray(L1_gnn_b)}
    nc = bacc.Bacc("TRN2", target_bir_lowering=False, num_devices=1)
    args = [nc.dram_tensor(name, a.shape, mybir.dt.from_np(a.dtype), kind="ExternalInput").ap()
            for name, a in arrays.items()]
    out = nc.dram_tensor("out_dram", (n, d), mybir.dt.float32, kind="ExternalOutput").ap()
    gnn_two_layer_kernel(nc, *args, out)
    r = run_bass_kernel_spmd(nc, [arrays], core_ids=[0])
    return r.results[0]["out_dram"]
```

```python
import concourse.bass as bass
from concourse import mybir
from contextlib import ExitStack


def gnn_two_layer_kernel(
    nc: bass.Bass,
    x: bass.AP,
    adj_t: bass.AP,
    w: bass.AP,
    b: bass.AP,
    out: bass.AP,
):
    fp32, fp16, u32 = mybir.dt.float32, mybir.dt.float16, mybir.dt.uint32
    ALU = mybir.AluOpType
    ACT = mybir.ActivationFunctionType
    AX = mybir.AxisListType

    P = 128
    N, D = x.shape
    UNITS = N // P
    KT = N // P
    CHUNKS = 4
    SUBS = 8
    KPC, KPS = KT // CHUNKS, KT // SUBS
    CW, SW = KPC * P, KPS * P
    RAW = 2 * CHUNKS
    RING = 4
    MASKED = (0, 1, 5)
    ADDED = tuple(s for s in range(SUBS) if s not in MASKED)
    BY_ACT = (0, 1, 4, 5)
    BY_DVE = tuple(s for s in range(SUBS) if s not in BY_ACT)
    NM, NA = len(MASKED), len(ADDED)
    AHEAD = SUBS + 2
    LOOK = SUBS + 2
    COUNT = AHEAD + 2
    TMP = 4
    EARLY = 2
    FIRST_MASKS = 3
    GX = KT // SUBS
    XH = [(a, z) for a, z in ((0, GX // 2), (GX // 2, GX)) if a < z]
    HS = 2048.0
    LN_EPS, NORM_EPS = 1e-5, 1e-12
    ONE = 2 * D
    HALF = UNITS // 2

    x_tiles = x.rearrange("(t p) d -> t p d", p=P)
    x_groups = x.rearrange("(g t p) d -> g p t d", p=P, t=GX)
    adj_rows = adj_t.rearrange("u c p f -> (u c p) f")
    x1_dram = nc.dram_tensor("x1_dram", [N, D], fp32, kind="Internal").ap()
    g_dram = nc.dram_tensor("g_dram", [N, 2 * D], fp16, kind="Internal").ap()
    g_chunks = g_dram.rearrange("(c t p) d -> c p t d", p=P, t=KPC)

    ctx = ExitStack()
    with ctx:
        def sb(name, shape, dt):
            return ctx.enter_context(nc.sbuf_tensor(name, shape, dt))

        def pb(name):
            return ctx.enter_context(nc.psum_tensor(name, [P, 512], fp32))

        def sem(name):
            return ctx.enter_context(nc.semaphore(name))

        H = sb("H", [P, KT, 2 * D + 2], fp16)
        raw = sb("raw", [P, RAW, CW], fp32)
        a_hi = sb("a_hi", [P, RING, SW], fp16)
        a_lo = sb("a_lo", [P, RING, SW], fp16)
        pos_keep = sb("pos_keep", [P, 2, NM, SW], fp16)
        pos_tmp = sb("pos_tmp", [P, TMP, SW], fp16)
        sign_tmp = sb("sign_tmp", [P, SW], fp16)
        abs_tmp = sb("abs_tmp", [P, SW], fp32)
        inc = sb("inc", [P, 2, SW], fp32)
        r_row = sb("r_row", [P, 2, P], fp32)
        asum = sb("asum", [P, 2, SUBS + 1], fp32)
        amax = sb("amax", [P, 2, SUBS + 1], fp32)
        am = sb("am", [P, 1], fp32)
        ebits = sb("ebits", [P, 1], u32)
        scale = sb("scale", [P, UNITS], fp32)
        sc_now = sb("sc_now", [P, 2], fp32)
        un_now = sb("un_now", [P, 2], fp32)
        stats = sb("stats", [P, GX, 6], fp32)
        mv = sb("mv", [P, GX, 2], fp32)
        nt = sb("nt", [P, GX], fp32)
        sd = sb("sd", [P, GX], fp32)
        nw = sb("nw", [P, GX], fp32)
        rs = sb("rs", [P, 2, GX], fp32)
        nb = sb("nb", [P, 2, GX], fp32)
        cnt = sb("cnt", [P, 1], fp32)
        cnt_sq = sb("cnt_sq", [P, 1], fp32)
        cnt_r0 = sb("cnt_r0", [P, 1], fp32)
        cnt_n = sb("cnt_n", [P, 1], fp32)
        cnt_r = sb("cnt_r", [P, 2], fp32)
        diag = sb("diag", [P, P], fp32)
        unscale = sb("unscale", [P, UNITS], fp32)
        cnt_t = sb("cnt_t", [P, UNITS], fp32)
        deg = sb("deg", [P, 1], fp32)
        deg_r = sb("deg_r", [P, 1], fp32)
        agg_f = sb("agg_f", [P, 1], fp32)
        self_f = sb("self_f", [P, 1], fp32)
        mean_t = sb("mean_t", [P, UNITS], fp32)
        rstd_t = sb("rstd_t", [P, UNITS], fp32)
        rden = sb("rden", [P, 1], fp32)
        st1 = sb("st1", [P, 6], fp32)
        mark = sb("mark", [P, 1], fp32)
        mv1 = sb("mv1", [P, 2], fp32)
        ve = sb("ve", [P, 1], fp32)
        ve_s = sb("ve_s", [P, 1], fp32)
        ve_r = sb("ve_r", [P, 1], fp32)
        ve_n = sb("ve_n", [P, 1], fp32)
        rs_g = sb("rs_g", [P, 1], fp32)
        ones_16 = sb("ones_16", [P, 2], fp16)
        ones_f = sb("ones_f", [P, P], fp32)
        ident = sb("ident", [P, P], fp32)

        xz = sb("xz", [P, max(3 * GX, 20) * D], fp32)
        xg = xz[:, 0:2 * GX * D].rearrange("p (b t d) -> p b t d", b=2, d=D)
        zt = xz[:, 2 * GX * D:3 * GX * D].rearrange("p (t d) -> p t d", d=D)
        taken = [0]

        def take(words):
            taken[0] += words
            return xz[:, taken[0] - words:taken[0]]

        x_in = take(2 * D).rearrange("p (b d) -> p b d", b=2)
        x1_o = take(2 * D).rearrange("p (b d) -> p b d", b=2)
        g_o = take(2 * D).bitcast(fp16).rearrange("p (b d) -> p b d", b=2)
        agg = take(D + 2)
        num = take(D + 2)
        z1 = take(D)
        hc = take(D)
        pooled = take(D)
        pooled_t = take(D)
        y = take(D)
        w_sb = take(D // P * D).rearrange("p (c d) -> p c d", d=D)
        b_sb = take(D)

        ps_a = [pb("ps_a0"), pb("ps_a1")]
        ps_m = [pb("ps_m0"), pb("ps_m1")]
        ps_c = [pb("ps_c0"), pb("ps_c1")]
        ps_r = pb("ps_r")
        ps_t, ps_o = ps_m

        raw_in = [sem(f"raw_in{i}") for i in range(RAW)]
        xg_in = [[sem(f"xg_in{i}_{h}") for h in range(len(XH))] for i in range(2)]
        x_in_got = [sem("x_in_got0"), sem("x_in_got1")]
        x1_st = [sem("x1_st0"), sem("x1_st1")]
        g_st = [sem("g_st0"), sem("g_st1")]
        g_in = [sem(f"g_in{i}") for i in range(CHUNKS)]
        w_in = sem("w_in")
        ident0 = sem("ident0")
        const_set = sem("const_set")
        ones_h = sem("ones_h")
        ln_step = sem("ln_step")
        ln_var = sem("ln_var")
        ln_sd = sem("ln_sd")
        ln_rs = sem("ln_rs")
        z_done = sem("z_done")
        h_hi = sem("h_hi")
        h_done = sem("h_done")
        abs_done = sem("abs_done")
        sign_done = sem("sign_done")
        mask_done = sem("mask_done")
        pos_done = sem("pos_done")
        counted = sem("counted")
        added = sem("added")
        deg_counted = sem("deg_counted")
        row_done = sem("row_done")
        deg_step = sem("deg_step")
        amax_done = sem("amax_done")
        sc_step = sem("sc_step")
        scale_done = sem("scale_done")
        cnt_done = sem("cnt_done")
        cnt_root = sem("cnt_root")
        cnt_step = sem("cnt_step")
        diag_done = sem("diag_done")
        r_mat = sem("r_mat")
        r_row_done = sem("r_row_done")
        half_done = sem("half_done")
        inc_done = sem("inc_done")
        hi_done = sem("hi_done")
        lo_done = sem("lo_done")
        sub_done = sem("sub_done")
        agg_done = sem("agg_done")
        num_done = sem("num_done")
        ep_step = sem("ep_step")
        x1_done = sem("x1_done")
        ve_done = sem("ve_done")
        ve_root = sem("ve_root")
        g_done = sem("g_done")
        pool_step = sem("pool_step")
        pool_done = sem("pool_done")
        tp_done = sem("tp_done")
        tc_done = sem("tc_done")
        o_done = sem("o_done")
        y_done = sem("y_done")
        res_done = sem("res_done")

        SIGNS0 = len(BY_ACT) * UNITS

        block = ctx.enter_context(nc.Block())

        def is_zero(v):
            return isinstance(v, int) and v == 0

        def sub_at(par, s):
            return raw[:, CHUNKS * par + s // 2, (s % 2) * SW:(s % 2 + 1) * SW]

        def pos_at(par, s):
            return pos_keep[:, par, MASKED.index(s), :] if s in MASKED else pos_tmp[:, s % TMP, :]

        @block.sync
        def _(sp):
            def load_chunk(v, j, src_unit, par, first=False):
                if not first:
                    sp.wait_ge(lo_done, SUBS * (v - 2) + 2 * j + 2)
                row = (src_unit * CHUNKS + j) * P
                sp.dma_start(raw[:, CHUNKS * par + j, :], adj_rows[bass.ds(row, P), :])\
                    .then_inc(raw_in[CHUNKS * par + j], 16)

            def load_xg(g):
                for h, (t0, t1) in enumerate(XH):
                    if g >= 2:
                        sp.wait_ge(z_done, GX * (g - 2) + t1)
                    sp.dma_start(xg[:, g % 2, t0:t1, :], x_groups[g][:, t0:t1, :]).then_inc(xg_in[g % 2][h], 16)

            load_xg(0)
            for j in range(CHUNKS):
                load_chunk(0, j, 0, 0, first=True)
                if j == 1:
                    load_xg(1)
            for j in range(CHUNKS):
                load_chunk(1, j, 1, 1, first=True)
            for g in range(2, SUBS):
                load_xg(g)

            def store0(u, par):
                sp.wait_ge(x1_done, u + 1)
                sp.dma_start(x1_dram[bass.ds(u * P, P), :], x1_o[:, par, :]).then_inc(x1_st[par], 16)
                sp.wait_ge(g_done, u + 1)
                sp.dma_start(g_dram[bass.ds(u * P, P), :], g_o[:, par, :]).then_inc(g_st[par], 16)

            def step0(u, par, first=False, wrap=False, last=False):
                for j in range(CHUNKS):
                    load_chunk(u + 2, j, u + 2 - UNITS if wrap else u + 2, par)
                if first:
                    sp.wait_ge(h_done, KT)
                    sp.dma_start(x_in[:, 0, :], x_tiles[0]).then_inc(x_in_got[0], 16)
                    sp.dma_start(w_sb[:, :, :], w.rearrange("(c p) n -> p c n", p=P)).then_inc(w_in, 16)
                    sp.dma_start(b_sb[:, :], b.partition_broadcast(P)).then_inc(w_in, 16)
                else:
                    store0(u - 1, 1 - par)
                if not last:
                    sp.dma_start(x_in[:, 1 - par, :], x[bass.ds((u + 1) * P, P), :])\
                        .then_inc(x_in_got[1 - par], 16)

            step0(0, 0, first=True)
            with nc.sync.Fori(0, HALF - 2) as i:
                step0(2 * i + 1, 1)
                step0(2 * i + 2, 0)
            step0(UNITS - 3, 1)
            step0(UNITS - 2, 0, wrap=True)
            step0(UNITS - 1, 1, wrap=True, last=True)

            for c in range(CHUNKS):
                if c == CHUNKS - 1:
                    store0(UNITS - 1, 1)
                sp.wait_ge(sub_done, SUBS * (UNITS - 1) + 2 * c + 2)
                for par in range(2):
                    sp.wait_ge(g_st[par], 16 * (KPC * (c + 1) // 2))
                sp.dma_start(H[:, c * KPC:(c + 1) * KPC, 0:2 * D], g_chunks[c]).then_inc(g_in[c], 16)
            for par in range(2):
                sp.wait_ge(x1_st[par], 16 * HALF)
                sp.dma_start(x_in[:, par, :], x1_dram[par * P:(par + 1) * P, :]).then_inc(x_in_got[par], 16)

            def store1(u, par):
                sp.wait_ge(res_done, u + 1)
                sp.dma_start(out[bass.ds(u * P, P), :], x1_o[:, par, :]).then_inc(x1_st[par], 16)

            def step1(u, par, first=False, more=True, last=False):
                if more:
                    for j in range(CHUNKS):
                        load_chunk(UNITS + u + 2, j, u + 2, par)
                if not first:
                    store1(u - 1, 1 - par)
                    if not last:
                        sp.dma_start(x_in[:, 1 - par, :], x1_dram[bass.ds((u + 1) * P, P), :])\
                            .then_inc(x_in_got[1 - par], 16)

            step1(0, 0, first=True)
            with nc.sync.Fori(0, HALF - 2) as i:
                step1(2 * i + 1, 1)
                step1(2 * i + 2, 0)
            step1(UNITS - 3, 1)
            step1(UNITS - 2, 0, more=False)
            step1(UNITS - 1, 1, more=False, last=True)
            store1(UNITS - 1, 1)
            for par in range(2):
                sp.wait_ge(x1_st[par], 16 * UNITS)
                sp.wait_ge(g_st[par], 16 * HALF)

        @block.gpsimd
        def _(pool):
            nc.gpsimd.memset(ident[:, :], 0.0).then_inc(ident0, 1)
            nc.gpsimd.memset(asum[:, :, SUBS:SUBS + 1], 1.0).then_inc(ident0, 1)
            nc.gpsimd.memset(ones_16[:, :], 1.0).then_inc(const_set, 1)
            nc.gpsimd.memset(ones_f[:, :], 1.0).then_inc(const_set, 1)
            nc.gpsimd.memset(H[:, :, ONE:ONE + 1], HS).then_inc(ones_h, 1)
            pool.wait_ge(ident0, 2)
            nc.gpsimd.affine_select(out=ident[:, :], in_=ident[:, :], compare_op=ALU.not_equal, fill=1.0,
                                    base=0, pattern=[[-1, P]], channel_multiplier=1).then_inc(const_set, 1)
            for u in range(UNITS):
                pool.wait_ge(abs_done, SUBS * (u + 1))
                nc.gpsimd.partition_all_reduce(amax[:, u % 2, :], asum[:, u % 2, :], P,
                                               bass.bass_isa.ReduceOp.max).then_inc(amax_done, 1)

        @block.scalar
        def _(act):
            def look(q, par, s, uses):
                if s % 2 == 0:
                    act.wait_ge(raw_in[CHUNKS * par + s // 2], 16 * uses)
                if s in BY_ACT:
                    nth = len(BY_ACT) * q + BY_ACT.index(s)
                    if not is_zero(nth):
                        act.wait_ge(mask_done, nth)
                    nc.scalar.activation(sign_tmp[:, :], sub_at(par, s), ACT.Sign).then_inc(sign_done, 1)
                if not is_zero(SUBS * q + s):
                    act.wait_ge(abs_done, SUBS * q + s)
                nc.scalar.activation(abs_tmp[:, :], sub_at(par, s), ACT.Abs,
                                     accum_out=asum[:, par, s:s + 1]).then_inc(abs_done, 1)
                if s in BY_ACT:
                    act.wait_ge(sign_done, nth + 1)
                    if s in ADDED and not (isinstance(q, int) and SUBS * q + s < TMP):
                        act.wait_ge(counted, SUBS * q + s - TMP + 1)
                    nc.scalar.activation(pos_at(par, s), sign_tmp[:, :], ACT.Relu).then_inc(mask_done, 1)

            def split_hi(v, par, s, src, free=True):
                if free:
                    act.wait_ge(sub_done, SUBS * v + s - RING + 1)
                nc.scalar.activation(a_hi[:, s % RING, :], src, ACT.Copy,
                                     scale=sc_now[:, par:par + 1]).then_inc(hi_done, 1)

            def roots(u):
                act.wait_ge(cnt_done, u + 1)
                nc.scalar.activation(cnt_sq[:, :], cnt[:, :], ACT.Sqrt).then_inc(cnt_root, 1)

            def ln_root(g):
                act.wait_ge(ln_var, g + 1)
                nc.scalar.activation(sd[:, :], nt[:, :], ACT.Sqrt).then_inc(ln_sd, 1)

            def features(g, t0, t1):
                act.wait_ge(ln_rs, 2 * (g + 1))
                for t in range(t0, t1 + 1):
                    n = g * GX + t
                    if t < t1:
                        if n >= GX:
                            act.wait_ge(h_done, n - GX + 1)
                        nc.scalar.activation(zt[:, t, :], xg[:, g % 2, t, :], ACT.Identity,
                                             bias=nb[:, g % 2, t:t + 1], scale=rs[:, g % 2, t:t + 1])\
                            .then_inc(z_done, 1)
                    if t > t0:
                        act.wait_ge(z_done, n)
                        nc.scalar.activation(H[:, n - 1, D:2 * D], zt[:, t - 1, :], ACT.Relu).then_inc(h_hi, 1)

            def group(g):
                mid = (GX + 1) // 2
                features(g, 0, mid)
                if g < SUBS - 1:
                    ln_root(g + 1)
                if mid < GX:
                    features(g, mid, GX)

            def epilogue0(u, par):
                act.wait_ge(sub_done, SUBS * (u + 1))
                if not is_zero(u):
                    act.wait_ge(num_done, u)
                nc.scalar.activation(agg[:, 0:D + 1], ps_a[par][:, 0:D + 1], ACT.Copy,
                                     scale=un_now[:, par:par + 1]).then_inc(agg_done, 1)

            def ve_roots(u):
                act.wait_ge(ve_done, u + 1)
                nc.scalar.activation(ve_s[:, :], ve[:, :], ACT.Sqrt).then_inc(ve_root, 1)

            def step0(u, par, half, first=False, ahead=SUBS):
                for s in range(SUBS):
                    if first and s + EARLY < SUBS:
                        group(s + EARLY)
                    def look_on():
                        if s < ahead:
                            over = (s + LOOK) // SUBS
                            look(u + over, (par + over) % 2, (s + LOOK) % SUBS,
                                 half + (par + over) // 2 + 1)

                    if s == 0:
                        act.wait_ge(scale_done, u + 1)
                    if s in ADDED:
                        look_on()
                        if s == 6 and not first:
                            ve_roots(u - 1)
                        if s == 6 and ahead:
                            roots(u + 1)
                        act.wait_ge(inc_done, NA * u + ADDED.index(s) + 1)
                        split_hi(u, par, s, inc[:, s % 2, :], free=not (first and s < RING))
                    else:
                        split_hi(u, par, s, sub_at(par, s), free=not (first and s < RING))
                        if s == 1:
                            act.wait_ge(r_mat, u + 1)
                            nc.scalar.activation(r_row[:, par, :], ps_r[:, 0:P], ACT.Copy).then_inc(r_row_done, 1)
                        look_on()
                    if s == RING - 1 and not first:
                        epilogue0(u - 1, 1 - par)

            ln_root(0)
            for m in range(LOOK):
                look(m // SUBS, m // SUBS, m % SUBS, 1)
                if m == FIRST_MASKS - 1:
                    group(0)
            roots(0)
            group(1)
            step0(0, 0, 0, first=True)
            step0(1, 1, 0)
            step0(2, 0, 1)
            with nc.scalar.Fori(1, HALF - 2) as i:
                step0(2 * i + 1, 1, i)
                step0(2 * i + 2, 0, i + 1)
            step0(UNITS - 3, 1, HALF - 2)
            step0(UNITS - 2, 0, HALF - 1, ahead=2 * SUBS - LOOK)
            step0(UNITS - 1, 1, HALF - 1, ahead=0)

            def turn(u):
                act.wait_ge(tp_done, u + 1)
                if not is_zero(u):
                    act.wait_ge(o_done, u)
                nc.scalar.activation(pooled_t[:, :], ps_t[:, 0:D], ACT.Copy).then_inc(tc_done, 1)

            def step1(u, par, uses, first=False):
                no_wait = isinstance(u, int) and u < 2
                act.wait_ge(scale_done, UNITS + u + 1)
                for s in range(SUBS):
                    if s % 2 == 0:
                        act.wait_ge(raw_in[CHUNKS * par + s // 2], 16 * uses)
                    if s == 0:
                        signs = pos_tmp[:, par, :]
                        if not no_wait:
                            act.wait_ge(deg_counted, u - 1)
                    else:
                        signs = pos_tmp[:, 2 + s % 2, :]
                        if s > 2:
                            act.wait_ge(added, (SUBS - 1) * u + s - 2)
                        elif not first:
                            act.wait_ge(added, (SUBS - 1) * u + 1 - s)
                    nc.scalar.activation(signs, sub_at(par, s), ACT.Sign).then_inc(sign_done, 1)
                    split_hi(UNITS + u, par, s, sub_at(par, s))
                    if s == RING - 1 and first:
                        epilogue0(UNITS - 1, 1)
                        ve_roots(UNITS - 1)
                    if s == SUBS - 2 and not first:
                        turn(u - 1)

            step1(0, 0, HALF + 1, first=True)
            step1(1, 1, HALF + 1)
            step1(2, 0, HALF + 2)
            with nc.scalar.Fori(1, HALF - 1) as i:
                step1(2 * i + 1, 1, HALF + i + 1)
                step1(2 * i + 2, 0, HALF + i + 2)
            step1(UNITS - 1, 1, UNITS)
            turn(UNITS - 1)

        @block.vector
        def _(dve):
            def link(ins, step_sem, count):
                ins.then_inc(step_sem, 1)
                dve.wait_ge(step_sem, count)

            def ln_stats(g):
                for h, (t0, t1) in enumerate(XH):
                    dve.wait_ge(xg_in[g % 2][h], 16 * (g // 2 + 1))
                    for t in range(t0, t1):
                        last = nc.vector.bn_stats(stats[:, t, :], xg[:, g % 2, t, :])
                link(last, ln_step, 6 * g + 1)
                for t in range(GX):
                    last = nc.vector.bn_aggr(mv[:, t, :], stats[:, t, :])
                link(last, ln_step, 6 * g + 2)
                nc.vector.tensor_scalar(nt[:, :], mv[:, :, 1], LN_EPS, None, ALU.add).then_inc(ln_var, 1)

            def ln_factors(g, part):
                r, n = rs[:, g % 2, :], nw[:, :]
                base = 6 * g + 2
                if part == 0:
                    dve.wait_ge(ln_sd, g + 1)
                    nc.vector.reciprocal(r, sd[:, :]).then_inc(ln_step, 1)
                if part == 1:
                    dve.wait_ge(ln_step, base + 1)
                    nc.vector.tensor_tensor(n, nt[:, :], r, ALU.mult).then_inc(ln_step, 1)
                if part == 2:
                    dve.wait_ge(ln_step, base + 2)
                    nc.vector.tensor_tensor(n, n, r, ALU.mult).then_inc(ln_step, 1)
                if part == 3:
                    dve.wait_ge(ln_step, base + 3)
                    nc.vector.tensor_scalar(n, n, -0.5 * HS, 1.5 * HS, ALU.mult, ALU.add).then_inc(ln_step, 1)
                if part == 4:
                    dve.wait_ge(ln_step, base + 4)
                    nc.vector.tensor_tensor(r, r, n, ALU.mult).then_inc(ln_rs, 1)
                if part == 5:
                    dve.wait_ge(ln_rs, 2 * g + 1)
                    nc.vector.scalar_tensor_tensor(out=nb[:, g % 2, :], in0=mv[:, :, 0], scalar=-1.0, in1=r,
                                                   op0=ALU.mult, op1=ALU.mult).then_inc(ln_rs, 1)

            def features_lo(g):
                for t in range(max(GX, 6)):
                    if t < GX:
                        n = g * GX + t
                        dve.wait_ge(h_hi, n + 1)
                        nc.vector.scalar_tensor_tensor(out=H[:, n, 0:D], in0=zt[:, t, :], scalar=0.0,
                                                       in1=H[:, n, D:2 * D], op0=ALU.max, op1=ALU.subtract)\
                            .then_inc(h_done, 1)
                    if t < 6 and g < SUBS - 1:
                        ln_factors(g + 1, t)

            def mask(q, par, s, uses):
                m = SUBS * q + s
                if s % 2 == 0 or s - 1 not in BY_DVE:
                    dve.wait_ge(raw_in[CHUNKS * par + s // 2], 16 * uses)
                if not (isinstance(m, int) and m < TMP):
                    dve.wait_ge(counted, m - TMP + 1)
                nc.vector.tensor_scalar(pos_at(par, s), sub_at(par, s), 0.0, None, ALU.is_gt)\
                    .then_inc(pos_done, 1)

            def find_scale(u, par, part):
                base = 2 * u
                if part == 0:
                    dve.wait_ge(amax_done, u + 1)
                    nc.vector.reduce_max(am[:, :], amax[:, par, :], AX.X).then_inc(sc_step, 1)
                if part == 1:
                    dve.wait_ge(sc_step, base + 1)
                    nc.vector.tensor_scalar(ebits[:, :], am[:, :].bitcast(u32), 0x7F800000, None,
                                            ALU.bitwise_and).then_inc(sc_step, 1)
                if part == 2:
                    dve.wait_ge(sc_step, base + 2)
                    nc.vector.tensor_scalar(un_now[:, par:par + 1].bitcast(u32), ebits[:, :],
                                            -float(13 << 23), None, ALU.add)
                    nc.vector.tensor_scalar(sc_now[:, par:par + 1].bitcast(u32), ebits[:, :], -1.0,
                                            float(267 << 23), ALU.mult, ALU.add).then_inc(scale_done, 1)

            def take_counts(u, par):
                dve.wait_ge(counted, SUBS * (u + 1))
                nc.vector.tensor_copy(cnt[:, :], ps_c[par][:, 0:1]).then_inc(cnt_done, 1)

            def find_rows(u, par, part):
                base = 5 * u
                r0, n, r = cnt_r0[:, :], cnt_n[:, :], cnt_r[:, par:par + 1]
                if part == 0:
                    dve.wait_ge(cnt_root, u + 1)
                    nc.vector.tensor_scalar(n, cnt_sq[:, :], NORM_EPS, None, ALU.max).then_inc(cnt_step, 1)
                if part == 1:
                    dve.wait_ge(cnt_step, base + 1)
                    nc.vector.reciprocal(r0, n).then_inc(cnt_step, 1)
                if part == 2:
                    dve.wait_ge(cnt_step, base + 2)
                    dve.wait_ge(cnt_done, u + 1)
                    nc.vector.scalar_tensor_tensor(out=n, in0=r0, scalar=cnt[:, :], in1=r0,
                                                   op0=ALU.mult, op1=ALU.mult).then_inc(cnt_step, 1)
                if part == 3:
                    dve.wait_ge(cnt_step, base + 3)
                    nc.vector.tensor_scalar(n, n, -0.5, 1.5, ALU.mult, ALU.add).then_inc(cnt_step, 1)
                if part == 4:
                    dve.wait_ge(cnt_step, base + 4)
                    nc.vector.tensor_tensor(r, r0, n, ALU.mult).then_inc(cnt_step, 1)
                if part == 5:
                    dve.wait_ge(cnt_step, base + 5)
                    nc.vector.tensor_scalar(diag[:, :], ident[:, :], r, None, ALU.mult)\
                        .then_inc(diag_done, 1)
                if part == 6:
                    dve.wait_ge(scale_done, u + 1)
                    nc.vector.tensor_copy(cnt_t[:, bass.ds(u, 1)], cnt[:, :])
                    nc.vector.tensor_copy(scale[:, bass.ds(u, 1)], sc_now[:, par:par + 1])
                    nc.vector.tensor_scalar(unscale[:, bass.ds(u, 1)], un_now[:, par:par + 1], 1.0 / HS,
                                            None, ALU.mult)

            def split_lo(v, par, s, src):
                dve.wait_ge(hi_done, SUBS * v + s + 1)
                nc.vector.scalar_tensor_tensor(out=a_lo[:, s % RING, :], in0=src,
                                               scalar=sc_now[:, par:par + 1], in1=a_hi[:, s % RING, :],
                                               op0=ALU.mult, op1=ALU.subtract).then_inc(lo_done, 1)

            def split_lo0(u, par, s):
                split_lo(u, par, s, inc[:, s % 2, :] if s in ADDED else sub_at(par, s))

            EP = 9

            def epilogue0(u, par, uses, part):
                base = EP * u
                again = not (isinstance(uses, int) and uses == 1)
                x1 = x1_o[:, par, :]
                if part == 0:
                    dve.wait_ge(sub_done, SUBS * (u + 1))
                    dve.wait_ge(agg_done, u + 1)
                    nc.vector.scalar_tensor_tensor(out=num[:, 0:D + 1], in0=ps_m[par][:, 0:D + 1],
                                                   scalar=cnt_r[:, par:par + 1], in1=agg[:, 0:D + 1],
                                                   op0=ALU.mult, op1=ALU.add).then_inc(num_done, 1)
                if part == 1:
                    dve.wait_ge(num_done, u + 1)
                    nc.vector.reciprocal(rden[:, :], num[:, D:D + 1]).then_inc(ep_step, 1)
                if part == 2:
                    dve.wait_ge(ep_step, base + 1)
                    dve.wait_ge(x_in_got[par], 16 * uses)
                    if again:
                        dve.wait_ge(x1_st[par], 16 * (uses - 1))
                    nc.vector.scalar_tensor_tensor(out=x1, in0=num[:, 0:D], scalar=rden[:, :],
                                                   in1=x_in[:, par, :], op0=ALU.mult, op1=ALU.add)\
                        .then_inc(x1_done, 1)
                if part == 3:
                    dve.wait_ge(x1_done, u + 1)
                    nc.vector.bn_stats(st1[:, :], x1).then_inc(ep_step, 1)
                if part == 4:
                    dve.wait_ge(ep_step, base + 2)
                    nc.vector.tensor_copy(mark[:, :], rden[:, :])
                    nc.vector.bn_aggr(mv1[:, :], st1[:, :]).then_inc(ep_step, 1)
                if part == 5:
                    dve.wait_ge(ep_step, base + 3)
                    nc.vector.tensor_scalar(ve[:, :], mv1[:, 1:2], LN_EPS, None, ALU.add).then_inc(ve_done, 1)
                    nc.vector.tensor_copy(mean_t[:, bass.ds(u, 1)], mv1[:, 0:1])
                if part == 6:
                    dve.wait_ge(ve_root, u + 1)
                    nc.vector.reciprocal(ve_r[:, :], ve_s[:, :]).then_inc(ep_step, 1)
                if part == 7:
                    dve.wait_ge(ep_step, base + 4)
                    nc.vector.scalar_tensor_tensor(out=ve_n[:, :], in0=ve[:, :], scalar=ve_r[:, :],
                                                   in1=ve_r[:, :], op0=ALU.mult, op1=ALU.mult)\
                        .then_inc(ep_step, 1)
                if part == 8:
                    dve.wait_ge(ep_step, base + 5)
                    nc.vector.tensor_scalar(ve_n[:, :], ve_n[:, :], -0.5, 1.5, ALU.mult, ALU.add)\
                        .then_inc(ep_step, 1)
                if part == 9:
                    dve.wait_ge(ep_step, base + 6)
                    nc.vector.tensor_tensor(rstd_t[:, bass.ds(u, 1)], ve_r[:, :], ve_n[:, :], ALU.mult)
                    nc.vector.scalar_tensor_tensor(out=rs_g[:, :], in0=ve_r[:, :], scalar=HS, in1=ve_n[:, :],
                                                   op0=ALU.mult, op1=ALU.mult).then_inc(ep_step, 1)
                if part == 10:
                    dve.wait_ge(ep_step, base + 7)
                    nc.vector.tensor_scalar(z1, x1, mv1[:, 0:1], rs_g[:, :], ALU.subtract, ALU.mult)\
                        .then_inc(ep_step, 1)
                if part == 11:
                    dve.wait_ge(ep_step, base + 8)
                    if again:
                        dve.wait_ge(g_st[par], 16 * (uses - 1))
                    nc.vector.tensor_scalar(g_o[:, par, D:2 * D], z1, 0.0, None, ALU.max)\
                        .then_inc(ep_step, 1)
                if part == 12:
                    dve.wait_ge(ep_step, base + 9)
                    nc.vector.scalar_tensor_tensor(out=g_o[:, par, 0:D], in0=z1, scalar=0.0,
                                                   in1=g_o[:, par, D:2 * D], op0=ALU.max, op1=ALU.subtract)\
                        .then_inc(g_done, 1)

            MASK, HALF_INC, LO, INC = range(4)
            BETWEEN = {
                (4, LO): [("end", 0)], (4, INC): [("end", 1)],
                (5, MASK): [("end", 2)], (5, LO): [("end", 3)],
                (6, MASK): [("end", 4)], (6, HALF_INC): [("end", 5)], (6, LO): [("counts", 0)],
                (6, INC): [("end", 6), ("scale", 0)],
                (7, MASK): [("end", 7), ("scale", 1), ("rows", 0)],
                (7, HALF_INC): [("end", 8), ("scale", 2), ("rows", 1)],
                (7, LO): [("end", 9), ("rows", 2)],
                (7, INC): [("rows", 3), ("end", 10), ("rows", 4), ("rows", 6), ("rows", 5), ("end", 11), ("end", 12)]}

            def step0(u, par, half, first=False, ahead=SUBS):
                def between(s, place):
                    for what, part in BETWEEN.get((s, place), []):
                        if what == "end" and not first:
                            epilogue0(u - 1, 1 - par, half + par, part)
                        if what == "counts" and ahead:
                            take_counts(u + 1, 1 - par)
                        if what == "scale" and ahead:
                            find_scale(u + 1, 1 - par, part)
                        if what == "rows" and ahead:
                            find_rows(u + 1, 1 - par, part)

                for s in range(SUBS):
                    n = SUBS * u + s
                    if first and s + EARLY < SUBS:
                        if s + EARLY < SUBS - 1:
                            ln_stats(s + EARLY + 1)
                        features_lo(s + EARLY)
                    if s < ahead and (s + AHEAD) % SUBS in BY_DVE:
                        over = (s + AHEAD) // SUBS
                        mask(u + over, (par + over) % 2, (s + AHEAD) % SUBS, half + (par + over) // 2 + 1)
                    between(s, MASK)
                    if s == ADDED[0]:
                        dve.wait_ge(r_row_done, u + 1)
                    if s in ADDED:
                        nth = NA * u + ADDED.index(s) + 1
                        now = inc[:, s % 2, :]
                        if not (first and s < ADDED[0] + 2):
                            dve.wait_ge(hi_done, n - 1)
                            dve.wait_ge(lo_done, n - 1)
                        nc.vector.scalar_tensor_tensor(
                            out=now.rearrange("p (k r) -> p k r", r=P),
                            in0=sub_at(par, s).rearrange("p (k r) -> p k r", r=P), scalar=0.0,
                            in1=r_row[:, par:par + 1, :].to_broadcast([P, KPS, P]),
                            op0=ALU.is_gt, op1=ALU.mult).then_inc(half_done, 1)
                        between(s, HALF_INC)
                    if s > 0:
                        split_lo0(u, par, s - 1)
                    elif not first:
                        split_lo0(u - 1, 1 - par, SUBS - 1)
                    between(s, LO)
                    if s in ADDED:
                        dve.wait_ge(half_done, nth)
                        nc.vector.tensor_tensor(now, now, sub_at(par, s), ALU.add).then_inc(inc_done, 1)
                        between(s, INC)

            ln_stats(0)
            for part in range(6):
                ln_factors(0, part)
            for m in range(AHEAD):
                if m % SUBS in BY_DVE:
                    mask(m // SUBS, m // SUBS, m % SUBS, 1)
                if m == FIRST_MASKS - 1:
                    ln_stats(1)
                    features_lo(0)
            dve.wait_ge(const_set, 3)
            take_counts(0, 0)
            for part in range(3):
                find_scale(0, 0, part)
            for part in range(7):
                find_rows(0, 0, part)
            ln_stats(2)
            features_lo(1)
            step0(0, 0, 0, first=True)
            step0(1, 1, 0)
            step0(2, 0, 1)
            with nc.vector.Fori(1, HALF - 2) as i:
                step0(2 * i + 1, 1, i)
                step0(2 * i + 2, 0, i + 1)
            step0(UNITS - 3, 1, HALF - 2)
            step0(UNITS - 2, 0, HALF - 1, ahead=2 * SUBS - AHEAD)
            step0(UNITS - 1, 1, HALF - 1, ahead=0)
            split_lo0(UNITS - 1, 1, SUBS - 1)

            def sum_signs(u, par, s):
                dve.wait_ge(sign_done, SIGNS0 + SUBS * u + s + 1)
                if s > 1:
                    dve.wait_ge(added, (SUBS - 1) * u + s - 1)
                nc.vector.tensor_tensor(pos_tmp[:, par, :], pos_tmp[:, par, :], pos_tmp[:, 2 + s % 2, :],
                                        ALU.add).then_inc(added, 1)

            def row_factors(u, par, part):
                base = 3 * u
                if part == 0:
                    dve.wait_ge(deg_counted, u + 1)
                    nc.vector.scalar_tensor_tensor(out=deg[:, :], in0=cnt_t[:, bass.ds(u, 1)], scalar=2.0,
                                                   in1=ps_c[par][:, 0:1], op0=ALU.mult, op1=ALU.subtract)\
                        .then_inc(deg_step, 1)
                if part == 1:
                    dve.wait_ge(deg_step, base + 1)
                    nc.vector.tensor_scalar(deg[:, :], deg[:, :], 1.0, None, ALU.max).then_inc(deg_step, 1)
                if part == 2:
                    dve.wait_ge(deg_step, base + 2)
                    nc.vector.reciprocal(deg_r[:, :], deg[:, :]).then_inc(deg_step, 1)
                if part == 3:
                    dve.wait_ge(deg_step, base + 3)
                    nc.vector.tensor_tensor(agg_f[:, :], deg_r[:, :], unscale[:, bass.ds(u, 1)], ALU.mult)
                    nc.vector.tensor_scalar(self_f[:, :], deg_r[:, :], 1.0, None, ALU.add).then_inc(row_done, 1)

            def pool_row(u, par, uses):
                base = 2 * u
                dve.wait_ge(x_in_got[par], 16 * uses)
                link(nc.vector.tensor_scalar(z1, x_in[:, par, :], mean_t[:, bass.ds(u, 1)],
                                             rstd_t[:, bass.ds(u, 1)], ALU.subtract, ALU.mult), pool_step, base + 1)
                dve.wait_ge(row_done, u + 1)
                link(nc.vector.tensor_scalar(hc, z1, 0.0, self_f[:, :], ALU.max, ALU.mult), pool_step, base + 2)
                dve.wait_ge(sub_done, SUBS * (UNITS + u + 1))
                if not is_zero(u):
                    dve.wait_ge(tp_done, u)
                nc.vector.scalar_tensor_tensor(out=pooled, in0=ps_a[par][:, 0:D],
                                               scalar=agg_f[:, :], in1=hc,
                                               op0=ALU.mult, op1=ALU.add).then_inc(pool_done, 1)

            def result(u, par, uses):
                dve.wait_ge(o_done, u + 1)
                link(nc.vector.tensor_tensor(y, ps_o[:, 0:D], b_sb, ALU.add), y_done, u + 1)
                dve.wait_ge(x1_st[par], 16 * (uses - 1))
                nc.vector.scalar_tensor_tensor(out=x1_o[:, par, :], in0=y, scalar=0.0, in1=x_in[:, par, :],
                                               op0=ALU.max, op1=ALU.add).then_inc(res_done, 1)

            def step1(u, par, uses, before=None):
                if before is not None:
                    dve.wait_ge(hi_done, SUBS * (UNITS + u - 1))
                link(nc.vector.tensor_copy(sc_now[:, par:par + 1], scale[:, bass.ds(u, 1)]),
                     scale_done, UNITS + u + 1)
                for s in range(SUBS):
                    if s % 2 == 0:
                        dve.wait_ge(raw_in[CHUNKS * par + s // 2], 16 * uses)
                    if s > 0:
                        sum_signs(u, par, s)
                    split_lo(UNITS + u, par, s, sub_at(par, s))
                    if s < 4 and before is not None:
                        row_factors(u - 1, 1 - par, s)
                    if s == RING - 1 and before is None:
                        for part in range(13):
                            epilogue0(UNITS - 1, 1, HALF, part)
                    elif s == RING - 1:
                        pool_row(u - 1, 1 - par, before)
                    if s == SUBS - 2 and before is not None:
                        result(u - 1, 1 - par, before)

            dve.wait_ge(w_in, 32)
            step1(0, 0, HALF + 1)
            step1(1, 1, HALF + 1, HALF + 1)
            step1(2, 0, HALF + 2, HALF + 1)
            with nc.vector.Fori(1, HALF - 1) as i:
                step1(2 * i + 1, 1, HALF + i + 1, HALF + i + 1)
                step1(2 * i + 2, 0, HALF + i + 2, HALF + i + 1)
            step1(UNITS - 1, 1, UNITS, UNITS)
            for part in range(4):
                row_factors(UNITS - 1, 1, part)
            pool_row(UNITS - 1, 1, UNITS)
            result(UNITS - 1, 1, UNITS)

        @block.tensor
        def _(pe):
            pe.wait_ge(ones_h, 1)
            pe.wait_ge(const_set, 3)

            def add_up(par, masks, begin, end):
                for k in range(KPS):
                    last = nc.tensor.matmul(ps_c[par][:, 0:1], masks[:, k * P:(k + 1) * P], ones_16[:, 0:1],
                                            start=(begin and k == 0), stop=(end and k == KPS - 1))
                return last

            def count(q, par, s):
                if s in BY_ACT:
                    pe.wait_ge(mask_done, len(BY_ACT) * q + BY_ACT.index(s) + 1)
                else:
                    pe.wait_ge(pos_done, len(BY_DVE) * q + BY_DVE.index(s) + 1)
                add_up(par, pos_at(par, s), s == 0, s == SUBS - 1).then_inc(counted, 1)

            def rows_over(u):
                pe.wait_ge(diag_done, u + 1)
                if not is_zero(u):
                    pe.wait_ge(r_row_done, u)
                nc.tensor.matmul(ps_r[:, 0:P], ones_f[:, :], diag[:, :], start=True, stop=True)\
                    .then_inc(r_mat, 1)

            def unit0(u, par, first=False, free=True, ahead=SUBS):
                if free:
                    pe.wait_ge(agg_done, u - 1)
                    pe.wait_ge(num_done, u - 1)
                PA, PM = ps_a[par], ps_m[par]
                for s in range(SUBS):
                    pe.wait_ge(lo_done, SUBS * u + s + 1)
                    for k in range(KPS):
                        kt = s * KPS + k
                        if first:
                            pe.wait_ge(h_done, kt + 1)
                        hi = a_hi[:, s % RING, k * P:(k + 1) * P]
                        lo = a_lo[:, s % RING, k * P:(k + 1) * P]
                        h_hi1, h_lo = H[:, kt, D:2 * D + 1], H[:, kt, 0:D]
                        nc.tensor.matmul(PA[:, 0:D + 1], hi, h_hi1, start=(kt == 0), stop=False)
                        nc.tensor.matmul(PA[:, 0:D], hi, h_lo, start=False, stop=False)
                        last = nc.tensor.matmul(PA[:, 0:D + 1], lo, h_hi1, start=False, stop=(kt == KT - 1))
                        if s in MASKED:
                            pos = pos_at(par, s)[:, k * P:(k + 1) * P]
                            end = kt == (MASKED[-1] + 1) * KPS - 1
                            nc.tensor.matmul(PM[:, 0:D + 1], pos, h_hi1, start=(kt == 0), stop=False)
                            last = nc.tensor.matmul(PM[:, 0:D], pos, h_lo, start=False, stop=end)
                    last.then_inc(sub_done, 1)
                    for c in (s - 1, s):
                        if s % 2 == 1 and c < ahead:
                            over = (c + COUNT) // SUBS
                            count(u + over, (par + over) % 2, (c + COUNT) % SUBS)
                    if s == 6 and ahead:
                        rows_over(u + 1)

            for m in range(COUNT):
                count(m // SUBS, m // SUBS, m % SUBS)
                if m == SUBS - 1:
                    rows_over(0)
            unit0(0, 0, first=True, free=False)
            unit0(1, 1, free=False)
            with nc.tensor.Fori(1, HALF - 1) as i:
                unit0(2 * i, 0)
                unit0(2 * i + 1, 1)
            unit0(UNITS - 2, 0, ahead=SUBS * 2 - COUNT)
            unit0(UNITS - 1, 1, ahead=0)

            def turn(u):
                pe.wait_ge(pool_done, u + 1)
                for c in range(D // P):
                    last = nc.tensor.transpose(ps_t[:, c * P:(c + 1) * P], pooled[:, c * P:(c + 1) * P], ident[:, :])
                last.then_inc(tp_done, 1)

            def dense(u):
                pe.wait_ge(tc_done, u + 1)
                if not is_zero(u):
                    pe.wait_ge(y_done, u)
                for c in range(D // P):
                    last = nc.tensor.matmul(ps_o[:, 0:D], pooled_t[:, c * P:(c + 1) * P], w_sb[:, c, :],
                                            start=(c == 0), stop=(c == D // P - 1))
                last.then_inc(o_done, 1)

            DEGREE_AT = SUBS - 3

            def unit1(u, par, first=False, free=True):
                if free:
                    pe.wait_ge(pool_done, u - 1)
                PA = ps_a[par]
                for s in range(SUBS):
                    if first and s % 2 == 0:
                        pe.wait_ge(g_in[s // 2], 16)
                    pe.wait_ge(lo_done, SUBS * (UNITS + u) + s + 1)
                    for k in range(KPS):
                        kt = s * KPS + k
                        hi = a_hi[:, s % RING, k * P:(k + 1) * P]
                        lo = a_lo[:, s % RING, k * P:(k + 1) * P]
                        nc.tensor.matmul(PA[:, 0:D], hi, H[:, kt, D:2 * D], start=(kt == 0), stop=False)
                        nc.tensor.matmul(PA[:, 0:D], hi, H[:, kt, 0:D], start=False, stop=False)
                        last = nc.tensor.matmul(PA[:, 0:D], lo, H[:, kt, D:2 * D], start=False,
                                                stop=(kt == KT - 1))
                    last.then_inc(sub_done, 1)
                    if s == DEGREE_AT:
                        pe.wait_ge(added, (SUBS - 1) * (u + 1))
                        add_up(par, pos_tmp[:, par, :], True, True).then_inc(deg_counted, 1)
                    if s == 2 and not first:
                        turn(u - 1)
                    if s == RING and not first:
                        dense(u - 1)

            pe.wait_ge(w_in, 32)
            pe.wait_ge(agg_done, UNITS - 1)
            pe.wait_ge(num_done, UNITS - 1)
            unit1(0, 0, first=True, free=False)
            pe.wait_ge(agg_done, UNITS)
            pe.wait_ge(num_done, UNITS)
            unit1(1, 1, free=False)
            with nc.tensor.Fori(1, HALF) as i:
                unit1(2 * i, 0)
                unit1(2 * i + 1, 1)
            turn(UNITS - 1)
            dense(UNITS - 1)


def kernel(x, adj, L1_gnn_W, L1_gnn_b):
    import numpy as np
    import concourse.bacc as bacc
    from concourse.bass_utils import run_bass_kernel_spmd

    P, CHUNKS = 128, 4
    x, adj = np.asarray(x), np.asarray(adj)
    n, d = x.shape
    kt = n // P
    adj_t = np.ascontiguousarray(
        adj.reshape(n // P, P, CHUNKS, kt // CHUNKS, P).transpose(0, 2, 4, 3, 1)
    ).reshape(n // P, CHUNKS, P, kt // CHUNKS * P)
    arrays = {"x_dram": x, "adj_dram": adj_t, "w_dram": np.asarray(L1_gnn_W), "b_dram": np.asarray(L1_gnn_b)}
    nc = bacc.Bacc("TRN2", target_bir_lowering=False, num_devices=1)
    args = [nc.dram_tensor(name, a.shape, mybir.dt.from_np(a.dtype), kind="ExternalInput").ap()
            for name, a in arrays.items()]
    out = nc.dram_tensor("out_dram", (n, d), mybir.dt.float32, kind="ExternalOutput").ap()
    gnn_two_layer_kernel(nc, *args, out)
    r = run_bass_kernel_spmd(nc, [arrays], core_ids=[0])
    return r.results[0]["out_dram"]
```
